# Optimizing a Trainium2 kernel written in Bass

```python
import numpy as np
import jax
import jax.numpy as jnp

def _softmax(x, axis=-1):
    return jax.nn.softmax(x, axis=axis)
def _gelu(x):
    return jax.nn.gelu(x, approximate=True)
def _silu(x):
    return jax.nn.silu(x)
def _sigmoid(x):
    return jax.nn.sigmoid(x)
def _layernorm(x, axis=-1, eps=1e-5):
    m = jnp.mean(x, axis=axis, keepdims=True)
    v = jnp.var(x, axis=axis, keepdims=True)
    return (x - m) / jnp.sqrt(v + eps)
def _scatter_add(tgt, idx, src, axis=0):
    return tgt.at[idx].add(src)
def _segment_sum(src, seg, n):
    return jax.ops.segment_sum(src, seg, n)

kernel_name = 'mk_conv_seq_d1_conv_nchw256_175c51'

def setup_inputs(seed: int = 0):
    np.random.seed(seed)
    _w = jnp.asarray
    def _rec_inputs():
        import jax
        import jax.numpy as jnp
        _gk = jax.random.key(seed)
        x = 7.22e-05 + 1 * jax.random.normal(jax.random.fold_in(_gk, 1), (8, 256, 64, 64), jnp.float32)
        return x
    x = _rec_inputs()
    def _L0_conv_setup():
        import jax, jax.numpy as jnp
        import numpy as np
        from jax import lax
        C = 256
        BN_EPS = 1e-05
        key = jax.random.key(seed)
        ks = jax.random.split(key, 8)
        N, H, W = (8, 64, 64)
        x = jax.random.normal(ks[0], (N, C, H, W), dtype=jnp.float32)
        wh = jax.random.normal(ks[1], (C, C), dtype=jnp.float32) * 0.02
        bh = jnp.zeros((C,), dtype=jnp.float32)
        ww = jax.random.normal(ks[2], (C, C), dtype=jnp.float32) * 0.02
        bw = jnp.zeros((C,), dtype=jnp.float32)
        conv_k = jax.random.normal(ks[3], (C, C, 3, 3), dtype=jnp.float32) * 0.02
        bn_w = jnp.ones((C,), dtype=jnp.float32)
        bn_b = jnp.zeros((C,), dtype=jnp.float32)
        bn_mean = jnp.zeros((C,), dtype=jnp.float32)
        bn_var = jnp.ones((C,), dtype=jnp.float32)
        gamma = jax.random.uniform(ks[4], (1,), dtype=jnp.float32)
        return {'x': x, 'wh': wh, 'bh': bh, 'ww': ww, 'bw': bw, 'conv_k': conv_k, 'bn_w': bn_w, 'bn_b': bn_b, 'bn_mean': bn_mean, 'bn_var': bn_var, 'gamma': gamma}
    _L0_conv_all = _L0_conv_setup()
    _L0_conv_in = {k: v for k, v in _L0_conv_all.items() if k in ('wh', 'bh', 'ww', 'bw', 'conv_k', 'bn_w', 'bn_b', 'bn_mean', 'bn_var', 'gamma', )}
    del _L0_conv_all

    return {
        "x": x,
        "L0_conv_wh": _L0_conv_in["wh"],
        "L0_conv_bh": _L0_conv_in["bh"],
        "L0_conv_ww": _L0_conv_in["ww"],
        "L0_conv_bw": _L0_conv_in["bw"],
        "L0_conv_conv_k": _L0_conv_in["conv_k"],
        "L0_conv_bn_w": _L0_conv_in["bn_w"],
        "L0_conv_bn_b": _L0_conv_in["bn_b"],
        "L0_conv_bn_mean": _L0_conv_in["bn_mean"],
        "L0_conv_bn_var": _L0_conv_in["bn_var"],
        "L0_conv_gamma": _L0_conv_in["gamma"],
    }

def reference(x, L0_conv_wh, L0_conv_bh, L0_conv_ww, L0_conv_bw, L0_conv_conv_k, L0_conv_bn_w, L0_conv_bn_b, L0_conv_bn_mean, L0_conv_bn_var, L0_conv_gamma):
    import jax
    import jax.numpy as jnp
    def _L0_conv_ref(x, wh, bh, ww, bw, conv_k, bn_w, bn_b, bn_mean, bn_var, gamma):
        import jax, jax.numpy as jnp
        import numpy as np
        from jax import lax
        C = 256
        BN_EPS = 1e-05
        N, Cc, H, W = x.shape
        x_h = jnp.transpose(x, (0, 3, 1, 2)).reshape(N * W, Cc, H)
        x_w = jnp.transpose(x, (0, 2, 1, 3)).reshape(N * H, Cc, W)
        xh_ = jnp.transpose(jnp.mean(x, axis=3), (0, 2, 1)) @ wh.T + bh
        xw_ = jnp.transpose(jnp.mean(x, axis=2), (0, 2, 1)) @ ww.T + bw
        att_h = jax.nn.softmax(jnp.matmul(x_h, jnp.tile(xh_, (W, 1, 1))), axis=-1)
        att_w = jax.nn.softmax(jnp.matmul(x_w, jnp.tile(xw_, (H, 1, 1))), axis=-1)
        out_h = jnp.transpose(jnp.matmul(att_h, x_h).reshape(N, W, Cc, H), (0, 2, 3, 1))
        out_w = jnp.transpose(jnp.matmul(att_w, x_w).reshape(N, H, Cc, W), (0, 2, 1, 3))
        out = gamma[0] * (out_h + out_w) + x
        y = lax.conv_general_dilated(out, conv_k, (1, 1), ((1, 1), (1, 1)), dimension_numbers=('NCHW', 'OIHW', 'NCHW'))
        inv = bn_w / jnp.sqrt(bn_var + BN_EPS)
        y = y * inv[:, None, None] + (bn_b - bn_mean * inv)[:, None, None]
        return jax.nn.relu(y)

    def _gn(v, G=32, eps=1e-5):
        B_, C_, H_, W_ = v.shape
        g = v.reshape(B_, G, C_ // G, H_, W_)
        m = jnp.mean(g, axis=(2, 3, 4), keepdims=True)
        s = jnp.var(g, axis=(2, 3, 4), keepdims=True)
        return ((g - m) / jnp.sqrt(s + eps)).reshape(v.shape)

    def _ln_c(v, eps=1e-6):
        m = jnp.mean(v, axis=1, keepdims=True)
        s = jnp.var(v, axis=1, keepdims=True)
        return (v - m) / jnp.sqrt(s + eps)

    def _ln_t(v, eps=1e-5):
        m = jnp.mean(v, axis=-1, keepdims=True)
        s = jnp.var(v, axis=-1, keepdims=True)
        return (v - m) / jnp.sqrt(s + eps)

    def _to_tokens(v):
        B_, C_, H_, W_ = v.shape
        return v.reshape(B_, C_, H_ * W_).transpose(0, 2, 1)
    def _from_tokens(t, like):
        B_, C_, H_, W_ = like.shape
        return t.transpose(0, 2, 1).reshape(B_, C_, H_, W_)

    x = _L0_conv_ref(x, L0_conv_wh, L0_conv_bh, L0_conv_ww, L0_conv_bw, L0_conv_conv_k, L0_conv_bn_w, L0_conv_bn_b, L0_conv_bn_mean, L0_conv_bn_var, L0_conv_gamma)
    return x


_drawn_inputs = setup_inputs


def setup_inputs(seed=0):
    import zlib

    import numpy as np

    out = dict(_drawn_inputs(seed))
    spreads = {'L0_conv_bh': (0.0, 0.703),
     'L0_conv_bw': (0.0, 0.629),
     'L0_conv_bn_w': (1.0, 0.2),
     'L0_conv_bn_b': (0.0, 0.1),
     'L0_conv_bn_mean': (0.0, 0.1),
     'L0_conv_bn_var': (1.0, 0.2)}
    factors = {'L0_conv_wh': 8.0, 'L0_conv_ww': 8.0}
    for name, (base, spread) in spreads.items():
        noise = np.random.default_rng([zlib.crc32(name.encode()), seed]).standard_normal(out[name].shape)
        drawn = base * np.exp(spread * noise) if base else spread * noise
        out[name] = jnp.asarray(drawn.astype(out[name].dtype))
    for name, factor in factors.items():
        out[name] = (out[name] * factor).astype(out[name].dtype)
    return out
```

```python
from contextlib import ExitStack

import concourse.bass as bass
from concourse import mybir

F32 = mybir.dt.float32
F32R = mybir.dt.float32r
ALU = mybir.AluOpType
ACT = mybir.ActivationFunctionType
AX = mybir.AxisListType

P = 128
N, C, H, W = 8, 256, 64, 64
CT = C // P
UPG = 4
ROWS = 2 * UPG
GROUPS = H // ROWS
DIR_UNITS = UPG * GROUPS
IMG_UNITS = 2 * DIR_UNITS
COMPS = 4
KW = 3
PAIRS = ROWS // 2
WP = W + 2
STEPS = 4
IMG_STEPS = STEPS * GROUPS
DMA = 16
CONV_BANKS = 2
FREE = 1
SMALL_LOADS = 6
BN_EPS = 1e-5
STEP_COMPS = ((1, 2), (0, 3))


def build(nc, x, wh_t, bh, ww_t, bw, conv_t, bn_params, gamma, out):
    ctx = ExitStack()
    with ctx:
        def sb(name, shape, dt=F32, stack=ctx):
            return stack.enter_context(nc.sbuf_tensor(name, shape, dt))

        def sem(name):
            return ctx.enter_context(nc.semaphore(name))

        image = sb("image", [P, CT, H + 2, W])
        rows = sb("rows", [P, 2, CT, ROWS, W])
        y_hi = sb("y_hi", [P, 2, N, C], F32R)
        y_lo = sb("y_lo", [P, 2, N, C], F32R)
        w_hi = sb("w_hi", [P, CT, COMPS, KW, C], F32R)
        w_lo = sb("w_lo", [P, CT, COMPS, KW, C], F32R)
        st_hl = sb("st_hl", [P, UPG, 2, CT, 2, H])
        st_x = sb("st_x", [P, UPG, 2, CT, H + 1])
        xt_sb = sb("xt_sb", [P, 2, 2, C], F32R)
        probs = sb("probs", [P, 2, CT, C])
        probs_t = sb("probs_t", [P, 4, CT, C])
        neg_max = sb("neg_max", [P, 4, CT])
        rcp = sb("rcp", [P, 2, 2 * CT])
        attn = sb("attn", [P, 2, 2 * CT, H])
        comp = sb("comp", [P, COMPS, CT, PAIRS, W])
        m1 = sb("m1", [P, PAIRS, W])
        m12_sum = sb("m12_sum", [P, PAIRS, W])
        m12_dif = sb("m12_dif", [P, PAIRS, W])
        y_rows = sb("y_rows", [P, PAIRS, 2, W])
        out_sb = sb("out_sb", [P, CT, ROWS, W])
        ident = sb("ident", [P, P])
        gam = sb("gam", [P, 1])
        bn = sb("bn", [P, 4, CT])
        bn_t = sb("bn_t", [P, 6, CT])
        bn_scale = sb("bn_scale", [P, CT])
        bn_bias = sb("bn_bias", [P, CT])
        with ExitStack() as early:
            conv_raw = sb("conv_raw", [P, CT, 3, KW * C], stack=early)
            proj = sb("proj", [P, 2, CT, C], stack=early)
            proj_b = sb("proj_b", [P, 2, C], stack=early)
            sums = sb("sums", [P, 2, CT, N, H], stack=early)
        v_hi = sb("v_hi", [P, 2, COMPS, CT, PAIRS, WP], F32R)
        v_lo = sb("v_lo", [P, 2, COMPS, CT, PAIRS, WP], F32R)

        def ps(name, shape):
            return ctx.enter_context(nc.psum_tensor(name, shape, F32))

        xt_ps = ps("xt_ps", [P, 2, C])
        scores = ps("scores", [P, 2, CT, C])
        pt_ps = ps("pt_ps", [P, 2, CT, C])
        prod = ps("prod", [P, 512])
        conv_ps = ps("conv_ps", [P, 2, 2, PAIRS, W])
        prod_v = prod[:, 0:2 * CT * (H + 1)].rearrange("p (k h) -> p k h", h=H + 1)

        weights_in, small_in, sums_in0, sums_in1 = (sem(s) for s in ("weights_in", "small_in", "sums_in0", "sums_in1"))
        image_in = sem("image_in")
        rows_in = [sem("rows_in0"), sem("rows_in1")]
        ident_ready, pads_ready, ones_ready = sem("ident_ready"), sem("pads_ready"), sem("ones_ready")
        summed, sums_twice, y_psum, y_ready = sem("summed"), sem("sums_twice"), sem("y_psum"), sem("y_ready")
        w_chain, w_ready = sem("w_chain"), sem("w_ready")
        bn_chain, bn_root, bn_ready = sem("bn_chain"), sem("bn_root"), sem("bn_ready")
        v_pads_ready = sem("v_pads_ready")
        x_staged, hi_staged, staged = sem("x_staged"), sem("hi_staged"), sem("staged")
        xt_done, xt_copied = sem("xt_done"), sem("xt_copied")
        scored, max_done, exp_done = sem("scored"), sem("max_done"), sem("exp_done")
        pt_done = sem("pt_done")
        pt_copied = [sem("pt_copied0"), sem("pt_copied1")]
        prod_done, rcp_done, normed, added = sem("prod_done"), sem("rcp_done"), sem("normed"), sem("added")
        comp_done, v_hi_done, v_lo_done = sem("comp_done"), sem("v_hi_done"), sem("v_lo_done")
        conv_done, m1_done, half_done, conv_taken = sem("conv_done"), sem("m1_done"), sem("half_done"), sem("conv_taken")
        relu_done = sem("relu_done")
        stored = [sem("stored0"), sem("stored1")]

        def by_tile(ap):
            return ap.rearrange("(t p) h w -> p t h w", p=P)

        block = ctx.enter_context(nc.Block())

        @block.sync
        def _(sp):
            for s in (image_in, *stored):
                sp.sem_inc(s, FREE)
            sp.dma_start(conv_raw[:], conv_t.rearrange("(t p) kh m -> p t kh m", p=P)).then_inc(weights_in, DMA)
            for d, w_ap in enumerate((wh_t, ww_t)):
                sp.dma_start(proj[:, d], w_ap.rearrange("(t p) c -> p t c", p=P)).then_inc(small_in, DMA)
            for d, b_ap in enumerate((bh, bw)):
                sp.dma_start(proj_b[:, d], b_ap.partition_broadcast(P)).then_inc(small_in, DMA)
            sp.dma_start(bn[:], bn_params).then_inc(small_in, DMA)
            sp.dma_start(gam[:], gamma.partition_broadcast(P)).then_inc(small_in, DMA)
            for i in range(N):
                for t in range(CT):
                    if i:
                        sp.wait_ge(summed, 2 * (CT * (i - 1) + t) + 2)
                    sp.dma_start(image[:, t, 1:H + 1, :], x[N - 1 - i].rearrange("(t p) h w -> t p h w", p=P)[t]) \
                        .then_inc((sums_in0, sums_in1)[t], DMA)

            def load_rows(n, g):
                sp.dma_start(rows[:, g % 2], by_tile(x[n])[:, :, ROWS * g:ROWS * g + ROWS, :]).then_inc(rows_in[g % 2], DMA)

            def one_image(n, last):
                for g in range(2):
                    if not (isinstance(n, int) and n == 0):
                        sp.wait_ge(staged, IMG_UNITS * n)
                        sp.wait_ge(x_staged, IMG_UNITS * n)
                    load_rows(n, g)
                for g in range(GROUPS + 2):
                    if g + 2 < GROUPS:
                        sp.wait_ge(staged, IMG_UNITS * n + DIR_UNITS + UPG * (g + 1))
                        sp.wait_ge(x_staged, IMG_UNITS * n + DIR_UNITS + UPG * (g + 1))
                        load_rows(n, g + 2)
                    loads = [g - 2] if 2 <= g < GROUPS else [GROUPS - 2, GROUPS - 1] if g == GROUPS else []
                    if loads and not last:
                        c = min(g - 1, GROUPS - 1)
                        sp.wait_ge(comp_done, COMPS * (GROUPS * n + c + 1))
                        for k in loads:
                            sp.dma_start(image[:, :, 1 + ROWS * k:1 + ROWS * (k + 1), :],
                                         by_tile(x[n + 1])[:, :, ROWS * k:ROWS * (k + 1), :]).then_inc(image_in, DMA)
                    if g >= 2:
                        for m in range(CT):
                            sp.wait_ge(relu_done, FREE + CT * (GROUPS * n + g - 2) + m + 1)
                            sp.dma_start(by_tile(out[n])[:, m, ROWS * (g - 2):ROWS * (g - 1), :], out_sb[:, m]) \
                                .then_inc(stored[m], DMA)

            one_image(0, False)
            with sp.Fori(1, N - 1) as n:
                one_image(n, False)
            one_image(N - 1, True)
            for m in range(CT):
                sp.wait_ge(stored[m], FREE + DMA * N * GROUPS)

        @block.gpsimd
        def _(pool):
            pool.sem_inc(v_lo_done, FREE)
            nc.gpsimd.memset(ident[:], 0.0).then_inc(w_chain, 1)
            pool.wait_ge(w_chain, 1)
            nc.gpsimd.affine_select(out=ident[:], in_=ident[:], compare_op=ALU.not_equal, fill=1.0, base=0,
                                    pattern=[[-1, P]], channel_multiplier=1).then_inc(ident_ready, 1)
            nc.gpsimd.memset(image[:, :, 0, :], 0.0)
            nc.gpsimd.memset(image[:, :, H + 1, :], 0.0).then_inc(pads_ready, 1)
            ones = nc.gpsimd.memset(st_x[:, :, :, :, H:H + 1].rearrange("p u j t o -> p (u j t) o"), 1.0)
            ones.then_inc(ones_ready, 1)

            pool.wait_ge(weights_in, DMA)
            count = [1]

            def link(ins):
                count[0] += 1
                ins.then_inc(w_chain, 1)
                pool.wait_ge(w_chain, count[0])

            def split_weights(t, c, w):
                hi, lo = (a[:, t, c].rearrange("p k c -> p (k c)") for a in (w_hi, w_lo))
                link(nc.gpsimd.tensor_scalar(hi, w, 1.0, 0.0, ALU.mult, ALU.add))
                return nc.gpsimd.tensor_tensor(lo, w, hi.bitcast(F32), ALU.subtract)

            for t in range(CT):
                g0, g1, g2 = (conv_raw[:, t, k] for k in range(3))
                split_weights(t, 0, g0)
                link(split_weights(t, 3, g2))
                link(nc.gpsimd.tensor_tensor(g0, g0, g2, ALU.add))
                link(nc.gpsimd.tensor_scalar(g0, g0, 0.5, 0.0, ALU.mult, ALU.add))
                link(nc.gpsimd.tensor_scalar(g1, g1, 0.5, 0.0, ALU.mult, ALU.add))
                link(nc.gpsimd.tensor_tensor(g2, g0, g1, ALU.subtract))
                split_weights(t, 2, g2)
                link(nc.gpsimd.tensor_tensor(g0, g0, g1, ALU.add))
                last = split_weights(t, 1, g0)
            last.then_inc(w_ready, 1)

            def split(u, p, src):
                pool.wait_ge(hi_staged, u + 1)
                nc.gpsimd.tensor_tensor(st_hl[:, p, :, :, 1, :], src, st_hl[:, p, :, :, 0, :],
                                        ALU.subtract).then_inc(staged, 1)

            def split_cols(u, p, w0):
                split(u, p, image[:, :, 1:H + 1, bass.ds(w0, 2)].rearrange("p t h j -> p j t h"))

            def split_rows(u, p, s):
                split(u, p, rows[:, s, :, 2 * p:2 * p + 2, :].rearrange("p t j w -> p j t w"))

            def add(u, s, dst):
                pool.wait_ge(normed, u + 1)
                a = attn[:, s].rearrange("p (j t) h -> p j t h", j=2)
                for j in range(2):
                    ins = nc.gpsimd.tensor_tensor(dst[:, j], dst[:, j], a[:, j], ALU.add)
                ins.then_inc(added, 1)

            def add_cols(u, s, w0):
                add(u, s, image[:, :, 1:H + 1, bass.ds(w0, 2)].rearrange("p t h j -> p j t h"))

            def add_rows(u, s, r0):
                add(u, s, image[:, :, bass.ds(r0 + 1, 2), :].rearrange("p t j w -> p j t w"))

            def lo_parts(before, s):
                for i in range(COMPS):
                    pool.wait_ge(v_hi_done, before + i + 1)
                    nc.gpsimd.tensor_tensor(v_lo[:, s, i, :, :, 1:W + 1], comp[:, i],
                                            v_hi[:, s, i, :, :, 1:W + 1].bitcast(F32), ALU.subtract).then_inc(v_lo_done, 1)

            pool.wait_ge(w_ready, 1)
            pool.wait_ge(summed, 2 * CT * N)
            pool.wait_ge(y_ready, 2 * N)
            for v in (v_hi, v_lo):
                vb = v[:].bitcast(F32).rearrange("p s i t r w -> p (s i t r) w")
                nc.gpsimd.memset(vb[:, :, 0:1], 0.0)
                pads = nc.gpsimd.memset(vb[:, :, WP - 1:WP], 0.0)
            pads.then_inc(v_pads_ready, 1)

            with pool.Fori(0, N) as n:
                u0 = IMG_UNITS * n
                v0 = u0 + DIR_UNITS
                chunks = GROUPS * n
                for p in range(UPG):
                    split_cols(u0 + p, p, 2 * p)
                with pool.Fori(0, GROUPS - 1) as g:
                    for p in range(UPG):
                        u = UPG * g + p
                        split_cols(u0 + u + UPG, p, 2 * (u + UPG))
                        add_cols(u0 + u, p % 2, 2 * u)
                for p in range(UPG):
                    u = DIR_UNITS - UPG + p
                    split_rows(v0 + p, p, 0)
                    add_cols(u0 + u, p % 2, 2 * u)

                def row_group(g, s, ahead=True, lo=True):
                    for p in range(UPG):
                        u = UPG * g + p
                        if ahead:
                            split_rows(v0 + u + UPG, p, 1 - s)
                        add_rows(v0 + u, p % 2, 2 * u)
                        if p == 0 and lo:
                            lo_parts(COMPS * (chunks + g - 1), 1 - s)

                pool.wait_ge(added, v0)
                row_group(0, 0, lo=False)
                with pool.Fori(0, GROUPS // 2 - 1) as h:
                    row_group(2 * h + 1, 1)
                    row_group(2 * h + 2, 0)
                row_group(GROUPS - 1, 1, ahead=False)
                lo_parts(COMPS * (chunks + GROUPS - 1), (GROUPS - 1) % 2)

        @block.scalar
        def _(act):
            act.sem_inc(relu_done, FREE)
            act.wait_ge(bn_chain, 1)
            nc.scalar.activation(bn_t[:, 1], bn_t[:, 0], ACT.Sqrt).then_inc(bn_root, 1)

            act.wait_ge(summed, 2 * CT * N)
            for d in range(2):
                for i in range(N):
                    k = d * N + i
                    if k >= 2:
                        act.wait_ge(y_psum, k - 1)
                    nc.scalar.copy(probs[:, k % 2, :, 0:2 * H].rearrange("p t (a h) -> p t a h", a=2),
                                   sums[:, d, :, i].unsqueeze(2).broadcast_to([P, CT, 2, H])).then_inc(sums_twice, 1)

            def copy_xt(u, s, start=False):
                act.wait_ge(xt_done, u + 1)
                if not start:
                    act.wait_ge(scored, 2 * (u - 2) + 2)
                nc.scalar.copy(xt_sb[:, s], xt_ps[:]).then_inc(xt_copied, 1)

            def exp(b, j, slot, start=False):
                act.wait_ge(max_done, b + 1)
                if not start:
                    act.wait_ge(pt_done, b - 1)
                for t in range(CT):
                    ins = nc.scalar.activation(probs[:, j, t], scores[:, j, t], ACT.Exp, bias=neg_max[:, slot, t:t + 1])
                ins.then_inc(exp_done, 1)

            def cols(w0):
                return image[:, :, 1:H + 1, bass.ds(w0, 2)].rearrange("p t h j -> p j t h")

            def rows_of(p, s):
                return rows[:, s, :, 2 * p:2 * p + 2, :].rearrange("p t j w -> p j t w")

            def stage_hi(u, p, src, start=False):
                if not start:
                    act.wait_ge(xt_done, u - UPG + 1)
                nc.scalar.copy(st_hl[:, p, :, :, 0, :].bitcast(F32R), src).then_inc(hi_staged, 1)

            def stage_x(u, p, src):
                nc.scalar.copy(st_x[:, p, :, :, 0:H], src).then_inc(x_staged, 1)

            def copy_pt(u, p, start=False):
                act.wait_ge(pt_done, 2 * u + 1)
                if not start:
                    act.wait_ge(prod_done, u - 1)
                nc.scalar.copy(probs_t[:, 2 * (p % 2)], pt_ps[:, 0]).then_inc(pt_copied[0], 1)

            def unit(u, p, x1, x2, first=False):
                start = first and p == 0
                if p % 2 == 0 and not start:
                    copy_pt(u - 1, p - 1, start=first)
                exp(2 * u, 0, 2 * (p % 2), start)
                if x1 is not None:
                    if not (first and p < UPG - 1):
                        act.wait_ge(prod_done, u - UPG + 2)
                    copy_xt(u + 1, (p + 1) % 2, start)
                    stage_x(u + 1, (p + 1) % UPG, x1)
                if x2 is not None:
                    stage_hi(u + 2, (p + 2) % UPG, x2, start=first and p < 2)
                exp(2 * u + 1, 1, 2 * (p % 2) + 1, start)

            def hi_parts(c, s):
                for i in range(COMPS):
                    act.wait_ge(comp_done, COMPS * c + i + 1)
                    nc.scalar.copy(v_hi[:, s, i, :, :, 1:W + 1], comp[:, i]).then_inc(v_hi_done, 1)

            def conv_step(c, q):
                m = q // 2
                if q % 2 == 0:
                    act.wait_ge(conv_done, STEPS * c + q + 1)
                    nc.scalar.copy(m1[:], conv_ps[:, 0, 0]).then_inc(m1_done, 1)
                else:
                    act.wait_ge(conv_taken, CONV_BANKS + STEPS * c + q + 1)
                    act.wait_ge(stored[m], FREE + DMA * c)
                    nc.scalar.activation(out_sb[:, m].rearrange("p (t r) w -> p t r w", r=2), y_rows[:], ACT.Relu,
                                         bias=bn_bias[:, m:m + 1], scale=bn_scale[:, m:m + 1]).then_inc(relu_done, 1)

            act.wait_ge(bn_ready, 1)
            act.wait_ge(v_pads_ready, 1)
            with act.Fori(0, N) as n:
                u0 = IMG_UNITS * n
                v0 = u0 + DIR_UNITS
                chunks = GROUPS * n
                loads = GROUPS // 2 * n
                act.wait_ge(image_in, FREE + DMA * GROUPS * n)
                for p in range(2):
                    stage_hi(u0 + p, p, cols(2 * p), start=True)
                stage_x(u0, 0, cols(0))
                copy_xt(u0, 0, start=True)
                for p in range(UPG):
                    unit(u0 + p, p, cols(2 * (p + 1)), cols(2 * (p + 2)), first=True)
                with act.Fori(1, GROUPS - 1) as g:
                    for p in range(UPG):
                        u = UPG * g + p
                        unit(u0 + u, p, cols(2 * (u + 1)), cols(2 * (u + 2)))
                for p in range(UPG):
                    u = DIR_UNITS - UPG + p
                    if p == 2:
                        act.wait_ge(rows_in[0], DMA * (loads + 1))
                    unit(u0 + u, p, cols(2 * (u + 1)) if p < 3 else rows_of(0, 0), cols(2 * (u + 2)) if p < 2 else rows_of(p - 2, 0))

                def row_group(g, s, next_loads, conv=True, split=True):
                    x = [rows_of(p, s) for p in range(UPG)] + [None if next_loads is None else rows_of(p, 1 - s) for p in range(2)]
                    for p in range(UPG):
                        if p == 2 and next_loads is not None:
                            act.wait_ge(rows_in[1 - s], DMA * next_loads)
                        unit(v0 + UPG * g + p, p, x[p + 1], x[p + 2])
                        if p == 2 and split:
                            hi_parts(chunks + g - 1, 1 - s)
                        if conv:
                            conv_step(chunks + g - 2, p)

                row_group(0, 0, loads + 1, conv=False, split=False)
                row_group(1, 1, loads + 2, conv=False)
                with act.Fori(1, GROUPS // 2 - 1) as h:
                    row_group(2 * h, 0, loads + h + 1)
                    row_group(2 * h + 1, 1, loads + h + 2)
                row_group(GROUPS - 2, 0, loads + GROUPS // 2)
                row_group(GROUPS - 1, 1, None)
                copy_pt(u0 + IMG_UNITS - 1, UPG - 1)
                hi_parts(chunks + GROUPS - 1, (GROUPS - 1) % 2)
                for c in (GROUPS - 2, GROUPS - 1):
                    for q in range(STEPS):
                        conv_step(chunks + c, q)

        @block.vector
        def _(dve):
            dve.wait_ge(small_in, SMALL_LOADS * DMA)
            root, r0, r1, half = (bn_t[:, i] for i in range(1, 5))
            count = [0]

            def link(ins):
                count[0] += 1
                ins.then_inc(bn_chain, 1)
                dve.wait_ge(bn_chain, count[0])

            link(nc.vector.tensor_scalar(bn_t[:, 0], bn[:, 3], BN_EPS, None, ALU.add))
            dve.wait_ge(bn_root, 1)
            link(nc.vector.reciprocal(r0, root))
            link(nc.vector.tensor_tensor(r1, bn_t[:, 0], r0, ALU.mult))
            link(nc.vector.tensor_tensor(half, r1, root, ALU.add))
            link(nc.vector.tensor_scalar(half, half, 0.5, None, ALU.mult))
            link(nc.vector.reciprocal(r0, half))
            link(nc.vector.tensor_tensor(bn_scale[:], bn[:, 0], r0, ALU.mult))
            link(nc.vector.tensor_tensor(r1, bn[:, 2], bn_scale[:], ALU.mult))
            nc.vector.tensor_tensor(bn_bias[:], bn[:, 1], r1, ALU.subtract).then_inc(bn_ready, 1)

            for i in range(N):
                for t in range(CT):
                    dve.wait_ge((sums_in0, sums_in1)[t], DMA * (i + 1))
                    half_image = image[:, t, 1:H + 1, :]
                    nc.vector.tensor_reduce(sums[:, 0, t, N - 1 - i], half_image, AX.X, ALU.add).then_inc(summed, 1)
                    nc.vector.tensor_reduce(sums[:, 1, t, N - 1 - i], half_image.rearrange("p h w -> p w h"),
                                            AX.X, ALU.add).then_inc(summed, 1)

            for d in range(2):
                for i in range(N):
                    k = d * N + i
                    dve.wait_ge(y_psum, k + 1)
                    y = attn[:, k % 2].rearrange("p k h -> p (k h)")
                    link(nc.vector.scalar_tensor_tensor(out=y, in0=scores[:, k % 2, 0], scalar=1.0 / W,
                                                        in1=proj_b[:, d], op0=ALU.mult, op1=ALU.add))
                    link(nc.vector.tensor_copy(y_hi[:, d, i], y))
                    nc.vector.tensor_tensor(y_lo[:, d, i], y, y_hi[:, d, i].bitcast(F32), ALU.subtract).then_inc(y_ready, 1)

            def maximum(b, j, slot):
                dve.wait_ge(scored, b + 1)
                nc.vector.tensor_reduce(neg_max[:, slot], scores[:, j], AX.X, ALU.max, negate=True).then_inc(max_done, 1)

            def copy_unit(u, p, j, start=False):
                dve.wait_ge(pt_done, 2 * u + j + 1)
                if not start:
                    dve.wait_ge(prod_done, u - 1)
                nc.vector.tensor_copy(probs_t[:, 2 * (p % 2) + j], pt_ps[:, j]).then_inc(pt_copied[j], 1)

            def norm(u, s, start=False):
                dve.wait_ge(prod_done, u + 1)
                nc.vector.reciprocal(rcp[:, s], prod_v[:, :, H]).then_inc(rcp_done, 1)
                if not start:
                    dve.wait_ge(added, u - 1)
                dve.wait_ge(rcp_done, u + 1)
                nc.vector.scalar_tensor_tensor(out=attn[:, s], in0=prod_v[:, :, 0:H], scalar=gam[:, 0:1],
                                               in1=rcp[:, s].unsqueeze(2).broadcast_to([P, 2 * CT, H]),
                                               op0=ALU.mult, op1=ALU.mult).then_inc(normed, 1)

            def unit(u, p, first=False):
                maximum(2 * u, 0, 2 * (p % 2))
                if not (first and p == 0) and p % 2:
                    copy_unit(u - 1, p - 1, 0, start=first and p < 3)
                if not (first and p < 2):
                    norm(u - 2, p % 2, start=first)
                maximum(2 * u + 1, 1, 2 * (p % 2) + 1)
                if not (first and p == 0):
                    copy_unit(u - 1, p - 1, 1, start=first and p < 3)

            def transform(c, r, u, base):
                dve.wait_ge(added, u)
                dve.wait_ge(v_lo_done, FREE + base)
                around = image[:, :, bass.ds(r, ROWS + 2), :]
                d = [around[:, :, i:i + ROWS - 1:2, :] for i in range(4)]
                for i, (a, b, op) in enumerate(((0, 2, ALU.subtract), (1, 2, ALU.add), (2, 1, ALU.subtract), (1, 3, ALU.subtract))):
                    nc.vector.tensor_tensor(comp[:, i], d[a], d[b], op).then_inc(comp_done, 1)

            def conv_step(c, q):
                m, k = q // 2, STEPS * c + q
                if q % 2 == 0:
                    dve.wait_ge(m1_done, CT * c + m + 1)
                    nc.vector.tensor_tensor(m12_sum[:], conv_ps[:, 0, 1], m1[:], ALU.add)
                    nc.vector.tensor_tensor(m12_dif[:], m1[:], conv_ps[:, 0, 1], ALU.subtract).then_inc(conv_taken, 1)
                else:
                    dve.wait_ge(conv_done, k + 1)
                    dve.wait_ge(conv_taken, CONV_BANKS + k)
                    dve.wait_ge(relu_done, FREE + CT * c + m)
                    nc.vector.tensor_tensor(y_rows[:, :, 0], conv_ps[:, 1, 0], m12_sum[:], ALU.add)
                    nc.vector.tensor_tensor(y_rows[:, :, 1], m12_dif[:], conv_ps[:, 1, 1], ALU.subtract).then_inc(conv_taken, 1)

            dve.sem_inc(conv_taken, CONV_BANKS)
            dve.wait_ge(pads_ready, 1)
            with dve.Fori(0, N) as n:
                u0 = IMG_UNITS * n
                v0 = u0 + DIR_UNITS
                chunks = GROUPS * n

                def transform_chunk(g):
                    transform(chunks + g, ROWS * g, v0 + UPG * (g + 1) + 1, COMPS * (chunks + g))

                for p in range(UPG):
                    unit(u0 + p, p, first=True)
                with dve.Fori(1, GROUPS + 1) as g:
                    for p in range(UPG):
                        unit(u0 + UPG * g + p, p)
                for p in range(UPG):
                    unit(v0 + UPG + p, p)
                    if p == 2:
                        transform_chunk(0)
                with dve.Fori(2, GROUPS) as g:
                    for p in range(UPG):
                        unit(v0 + UPG * g + p, p)
                        if p == 2:
                            transform_chunk(g - 1)
                        conv_step(chunks + g - 2, p)
                last = u0 + IMG_UNITS - 1
                norm(last - 1, 0)
                copy_unit(last, UPG - 1, 1)
                norm(last, 1)
                transform(chunks + GROUPS - 1, ROWS * (GROUPS - 1), last + 1, COMPS * (chunks + GROUPS - 1))
                for c in (GROUPS - 2, GROUPS - 1):
                    for q in range(STEPS):
                        conv_step(chunks + c, q)

        @block.tensor
        def _(pe):
            pe.wait_ge(small_in, SMALL_LOADS * DMA)
            for d in range(2):
                for i in range(N):
                    k = d * N + i
                    pe.wait_ge(sums_twice, k + 1)
                    if k >= 2:
                        pe.wait_ge(y_ready, k - 1)
                    for t in range(CT):
                        ins = nc.tensor.matmul(scores[:, k % 2, 0], probs[:, k % 2, t, 0:2 * H], proj[:, d, t], start=t == 0, stop=t == CT - 1)
                    ins.then_inc(y_psum, 1)
            pe.wait_ge(ident_ready, 1)
            pe.wait_ge(ones_ready, 1)
            pe.wait_ge(w_ready, 1)
            pe.wait_ge(y_ready, 2 * N)

            def transpose_x(u, p, start=False):
                pe.wait_ge(staged, u + 1)
                if not start:
                    pe.wait_ge(xt_copied, u)
                for j in range(2):
                    for t in range(CT):
                        ins = nc.tensor.transpose(xt_ps[:, j, t * P:(t + 1) * P],
                                                  st_hl[:, p, j, t].rearrange("p a h -> p (a h)"), ident[:])
                ins.then_inc(xt_done, 1)

            def score(u, p, j, d, start=False):
                pe.wait_ge(xt_copied, u + 1)
                if not start:
                    pe.wait_ge(exp_done, 2 * u + j - 1)
                for t in range(CT):
                    for y, flag in ((y_hi, True), (y_lo, False)):
                        ins = nc.tensor.matmul(scores[:, j, t], xt_sb[:, p % 2, j, t * P:(t + 1) * P],
                                               y[:, d, 2 * p + j], start=flag, stop=not flag)
                ins.then_inc(scored, 1)

            def transpose_p(u, j, start=False):
                pe.wait_ge(exp_done, 2 * u + j + 1)
                if not start:
                    pe.wait_ge(pt_copied[j], u)
                for t in range(CT):
                    for k in range(CT):
                        ins = nc.tensor.transpose(pt_ps[:, j, k, t * P:(t + 1) * P],
                                                  probs[:, j, t, k * P:(k + 1) * P], ident[:])
                ins.then_inc(pt_done, 1)

            def product(u, p, start=False):
                pe.wait_ge(x_staged, u + 1)
                if not start:
                    pe.wait_ge(normed, u)
                for j in range(2):
                    pe.wait_ge(pt_copied[j], u + 1)
                    for t in range(CT):
                        for k in range(CT):
                            ins = nc.tensor.matmul(prod_v[:, CT * j + t, :],
                                                   probs_t[:, 2 * (p % 2) + j, k, t * P:(t + 1) * P],
                                                   st_x[:, p, j, k, :], start=k == 0, stop=k == CT - 1)
                ins.then_inc(prod_done, 1)

            def unit(u, p, d, first=False, ahead=True):
                start, before = first and p == 0, not (first and p == 0)
                score(u, p, 0, d, start)
                if before:
                    transpose_p(u - 1, 0, start=first and p == 1)
                if ahead:
                    transpose_x(u + 1, (p + 1) % UPG)
                if not (first and p < 2):
                    product(u - 2, (p - 2) % UPG, start=first and p == 2)
                score(u, p, 1, d, start)
                if before:
                    transpose_p(u - 1, 1, start=first and p == 1)

            def conv_step(c, q, s):
                m, half, k = q // 2, q % 2, STEPS * c + q
                if q == 0:
                    pe.wait_ge(v_lo_done, FREE + COMPS * (c + 1))
                pe.wait_ge(conv_taken, CONV_BANKS + k - 1)
                for b, i in enumerate(STEP_COMPS[half]):
                    parts = [(t, kw, w, v) for t in range(CT) for kw in range(KW)
                             for w, v in ((w_hi, v_hi), (w_hi, v_lo), (w_lo, v_hi))]
                    for a, (t, kw, w, v) in enumerate(parts):
                        ins = nc.tensor.matmul(conv_ps[:, half, b], w[:, t, i, kw, m * P:(m + 1) * P],
                                               v[:, s, i, t, :, kw:kw + W], start=a == 0, stop=a == len(parts) - 1)
                ins.then_inc(conv_done, 1)

            with pe.Fori(0, N) as n:
                u0 = IMG_UNITS * n
                v0 = u0 + DIR_UNITS
                chunks = GROUPS * n
                transpose_x(u0, 0, start=True)
                for p in range(UPG):
                    unit(u0 + p, p, 0, first=True)
                with pe.Fori(1, GROUPS) as g:
                    for p in range(UPG):
                        unit(u0 + UPG * g + p, p, 0)
                with pe.Fori(0, 2) as g:
                    for p in range(UPG):
                        unit(v0 + UPG * g + p, p, 1)

                def row_group(g, s, last=False):
                    for p in range(UPG):
                        unit(v0 + UPG * g + p, p, 1, ahead=not (last and p == UPG - 1))
                        conv_step(chunks + g - 2, p, s)

                with pe.Fori(1, GROUPS // 2 - 1) as h:
                    row_group(2 * h, 0)
                    row_group(2 * h + 1, 1)
                row_group(GROUPS - 2, 0)
                row_group(GROUPS - 1, 1, last=True)
                last = u0 + IMG_UNITS - 1
                product(last - 1, UPG - 2)
                transpose_p(last, 0)
                transpose_p(last, 1)
                product(last, UPG - 1)
                for c in (GROUPS - 2, GROUPS - 1):
                    for q in range(STEPS):
                        conv_step(chunks + c, q, c % 2)


def kernel(x, L0_conv_wh, L0_conv_bh, L0_conv_ww, L0_conv_bw, L0_conv_conv_k, L0_conv_bn_w, L0_conv_bn_b,
           L0_conv_bn_mean, L0_conv_bn_var, L0_conv_gamma):
    import concourse.bacc as bacc
    import numpy as np
    from concourse.bass_utils import run_bass_kernel_spmd

    arrays = {
        "x": np.ascontiguousarray(x),
        "wh_t": np.ascontiguousarray(np.asarray(L0_conv_wh).T),
        "bh": np.ascontiguousarray(L0_conv_bh),
        "ww_t": np.ascontiguousarray(np.asarray(L0_conv_ww).T),
        "bw": np.ascontiguousarray(L0_conv_bw),
        "conv_t": np.ascontiguousarray(np.asarray(L0_conv_conv_k).transpose(1, 2, 3, 0)).reshape(C, 3, KW * C),
        "bn_params": np.ascontiguousarray(np.stack([L0_conv_bn_w, L0_conv_bn_b, L0_conv_bn_mean, L0_conv_bn_var])
                                          .reshape(4, CT, P).transpose(2, 0, 1)),
        "gamma": np.ascontiguousarray(L0_conv_gamma),
    }
    nc = bacc.Bacc("TRN2", target_bir_lowering=False, num_devices=1)
    aps = {name: nc.dram_tensor(name, a.shape, mybir.dt.from_np(a.dtype), kind="ExternalInput").ap()
           for name, a in arrays.items()}
    out = nc.dram_tensor("out", (N, C, H, W), F32, kind="ExternalOutput").ap()
    build(nc, **aps, out=out)
    result = run_bass_kernel_spmd(nc, [arrays], core_ids=[0])
    return result.results[0]["out"]
```

```python
from contextlib import ExitStack

import concourse.bass as bass
from concourse import mybir

F32 = mybir.dt.float32
F32R = mybir.dt.float32r
ALU = mybir.AluOpType
ACT = mybir.ActivationFunctionType
AX = mybir.AxisListType

P = 128
N, C, H, W = 8, 256, 64, 64
CT = C // P
UPG = 4
ROWS = 2 * UPG
GROUPS = H // ROWS
DIR_UNITS = UPG * GROUPS
IMG_UNITS = 2 * DIR_UNITS
COMPS = 4
KW = 3
PAIRS = ROWS // 2
WP = W + 2
STEPS = 4
IMG_STEPS = STEPS * GROUPS
DMA = 16
CONV_BANKS = 2
FREE = 1
SMALL_LOADS = 6
BN_EPS = 1e-5
STEP_COMPS = ((1, 2), (0, 3))


def build(nc, x, wh_t, bh, ww_t, bw, conv_t, bn_params, gamma, out):
    ctx = ExitStack()
    with ctx:
        def sb(name, shape, dt=F32, stack=ctx):
            return stack.enter_context(nc.sbuf_tensor(name, shape, dt))

        def sem(name):
            return ctx.enter_context(nc.semaphore(name))

        image = sb("image", [P, CT, H + 2, W])
        rows = sb("rows", [P, 2, CT, ROWS, W])
        y_hi = sb("y_hi", [P, 2, N, C], F32R)
        y_lo = sb("y_lo", [P, 2, N, C], F32R)
        w_hi = sb("w_hi", [P, CT, COMPS, KW, C], F32R)
        w_lo = sb("w_lo", [P, CT, COMPS, KW, C], F32R)
        st_x = sb("st_x", [P, UPG, CT, 2 * H + 2])
        xt_sb = sb("xt_sb", [P, 2, 2, C], F32R)
        probs = sb("probs", [P, 2, CT, C])
        probs_t = sb("probs_t", [P, 4, CT, C])
        neg_max = sb("neg_max", [P, 4, CT])
        rcp = sb("rcp", [P, 2, CT, 2])
        attn = sb("attn", [P, 2, CT, 2, H])
        comp = sb("comp", [P, COMPS, CT, PAIRS, W])
        m1 = sb("m1", [P, PAIRS, W])
        m12_sum = sb("m12_sum", [P, PAIRS, W])
        m12_dif = sb("m12_dif", [P, PAIRS, W])
        y_rows = sb("y_rows", [P, PAIRS, 2, W])
        out_sb = sb("out_sb", [P, CT, ROWS, W])
        ident = sb("ident", [P, P])
        gam = sb("gam", [P, 1])
        bn = sb("bn", [P, 4, CT])
        bn_t = sb("bn_t", [P, 6, CT])
        bn_scale = sb("bn_scale", [P, CT])
        bn_bias = sb("bn_bias", [P, CT])
        with ExitStack() as early:
            conv_raw = sb("conv_raw", [P, CT, 3, KW * C], stack=early)
            proj = sb("proj", [P, 2, CT, C], stack=early)
            proj_b = sb("proj_b", [P, 2, C], stack=early)
            sums = sb("sums", [P, 2, CT, N, H], stack=early)
        v_hi = sb("v_hi", [P, 2, COMPS, CT, PAIRS, WP], F32R)
        v_lo = sb("v_lo", [P, 2, COMPS, CT, PAIRS, WP], F32R)

        def ps(name, shape):
            return ctx.enter_context(nc.psum_tensor(name, shape, F32))

        xt_ps = ps("xt_ps", [P, 512])
        scores = ps("scores", [P, 2, CT, C])
        pt_ps = ps("pt_ps", [P, 2, CT, C])
        prod = ps("prod", [P, 512])
        conv_ps = ps("conv_ps", [P, 2, 2, PAIRS, W])
        prod_v = prod[:, 0:CT * (2 * H + 2)].rearrange("p (t c) -> p t c", t=CT)

        weights_in, small_in, sums_in0, sums_in1 = (sem(s) for s in ("weights_in", "small_in", "sums_in0", "sums_in1"))
        image_in = sem("image_in")
        rows_in = [sem("rows_in0"), sem("rows_in1")]
        ident_ready, pads_ready, ones_ready = sem("ident_ready"), sem("pads_ready"), sem("ones_ready")
        summed, sums_twice, y_psum, y_ready = sem("summed"), sem("sums_twice"), sem("y_psum"), sem("y_ready")
        w_chain, w_ready = sem("w_chain"), sem("w_ready")
        bn_chain, bn_root, bn_ready = sem("bn_chain"), sem("bn_root"), sem("bn_ready")
        v_pads_ready = sem("v_pads_ready")
        staged, xt_done, hi_copied, xt_ready = sem("staged"), sem("xt_done"), sem("hi_copied"), sem("xt_ready")
        scored, max_done, exp_done = sem("scored"), sem("max_done"), sem("exp_done")
        pt_done = sem("pt_done")
        pt_copied = [sem("pt_copied0"), sem("pt_copied1")]
        prod_done, rcp_done, normed, added = sem("prod_done"), sem("rcp_done"), sem("normed"), sem("added")
        comp_done, v_hi_done, v_lo_done = sem("comp_done"), sem("v_hi_done"), sem("v_lo_done")
        conv_done, m1_done, half_done, conv_taken = sem("conv_done"), sem("m1_done"), sem("half_done"), sem("conv_taken")
        relu_done = sem("relu_done")
        stored = [sem("stored0"), sem("stored1")]

        def by_tile(ap):
            return ap.rearrange("(t p) h w -> p t h w", p=P)

        block = ctx.enter_context(nc.Block())

        @block.sync
        def _(sp):
            for s in (image_in, *stored):
                sp.sem_inc(s, FREE)
            sp.dma_start(conv_raw[:], conv_t.rearrange("(t p) kh m -> p t kh m", p=P)).then_inc(weights_in, DMA)
            for d, w_ap in enumerate((wh_t, ww_t)):
                sp.dma_start(proj[:, d], w_ap.rearrange("(t p) c -> p t c", p=P)).then_inc(small_in, DMA)
            for d, b_ap in enumerate((bh, bw)):
                sp.dma_start(proj_b[:, d], b_ap.partition_broadcast(P)).then_inc(small_in, DMA)
            sp.dma_start(bn[:], bn_params).then_inc(small_in, DMA)
            sp.dma_start(gam[:], gamma.partition_broadcast(P)).then_inc(small_in, DMA)
            for i in range(N):
                for t in range(CT):
                    if i:
                        sp.wait_ge(summed, 2 * (CT * (i - 1) + t) + 2)
                    sp.dma_start(image[:, t, 1:H + 1, :], x[N - 1 - i].rearrange("(t p) h w -> t p h w", p=P)[t]) \
                        .then_inc((sums_in0, sums_in1)[t], DMA)

            def load_rows(n, g):
                sp.dma_start(rows[:, g % 2], by_tile(x[n])[:, :, ROWS * g:ROWS * g + ROWS, :]).then_inc(rows_in[g % 2], DMA)

            def one_image(n, last):
                for g in range(2):
                    if not (isinstance(n, int) and n == 0):
                        sp.wait_ge(staged, IMG_UNITS * n)
                    load_rows(n, g)
                for g in range(GROUPS + 2):
                    if g + 2 < GROUPS:
                        sp.wait_ge(staged, IMG_UNITS * n + DIR_UNITS + UPG * (g + 1))
                        load_rows(n, g + 2)
                    loads = [g - 2] if 2 <= g < GROUPS else [GROUPS - 2, GROUPS - 1] if g == GROUPS else []
                    if loads and not last:
                        c = min(g - 1, GROUPS - 1)
                        sp.wait_ge(comp_done, COMPS * (GROUPS * n + c + 1))
                        for k in loads:
                            sp.dma_start(image[:, :, 1 + ROWS * k:1 + ROWS * (k + 1), :],
                                         by_tile(x[n + 1])[:, :, ROWS * k:ROWS * (k + 1), :]).then_inc(image_in, DMA)
                    if g >= 2:
                        for m in range(CT):
                            sp.wait_ge(relu_done, FREE + CT * (GROUPS * n + g - 2) + m + 1)
                            sp.dma_start(by_tile(out[n])[:, m, ROWS * (g - 2):ROWS * (g - 1), :], out_sb[:, m]) \
                                .then_inc(stored[m], DMA)

            one_image(0, False)
            with sp.Fori(1, N - 1) as n:
                one_image(n, False)
            one_image(N - 1, True)
            for m in range(CT):
                sp.wait_ge(stored[m], FREE + DMA * N * GROUPS)

        @block.gpsimd
        def _(pool):
            pool.sem_inc(v_lo_done, FREE)
            nc.gpsimd.memset(ident[:], 0.0).then_inc(w_chain, 1)
            pool.wait_ge(w_chain, 1)
            nc.gpsimd.affine_select(out=ident[:], in_=ident[:], compare_op=ALU.not_equal, fill=1.0, base=0,
                                    pattern=[[-1, P]], channel_multiplier=1).then_inc(ident_ready, 1)
            nc.gpsimd.memset(image[:, :, 0, :], 0.0)
            nc.gpsimd.memset(image[:, :, H + 1, :], 0.0).then_inc(pads_ready, 1)
            ones = nc.gpsimd.memset(st_x[:].rearrange("p u t c -> p (u t) c")[:, :, 0:2 * H + 2:2 * H + 1], 1.0)
            ones.then_inc(ones_ready, 1)

            pool.wait_ge(weights_in, DMA)
            count = [1]

            def link(ins):
                count[0] += 1
                ins.then_inc(w_chain, 1)
                pool.wait_ge(w_chain, count[0])

            def split_weights(t, c, w):
                hi, lo = (a[:, t, c].rearrange("p k c -> p (k c)") for a in (w_hi, w_lo))
                link(nc.gpsimd.tensor_scalar(hi, w, 1.0, 0.0, ALU.mult, ALU.add))
                return nc.gpsimd.tensor_tensor(lo, w, hi.bitcast(F32), ALU.subtract)

            for t in range(CT):
                g0, g1, g2 = (conv_raw[:, t, k] for k in range(3))
                split_weights(t, 0, g0)
                link(split_weights(t, 3, g2))
                link(nc.gpsimd.tensor_tensor(g0, g0, g2, ALU.add))
                link(nc.gpsimd.tensor_scalar(g0, g0, 0.5, 0.0, ALU.mult, ALU.add))
                link(nc.gpsimd.tensor_scalar(g1, g1, 0.5, 0.0, ALU.mult, ALU.add))
                link(nc.gpsimd.tensor_tensor(g2, g0, g1, ALU.subtract))
                split_weights(t, 2, g2)
                link(nc.gpsimd.tensor_tensor(g0, g0, g1, ALU.add))
                last = split_weights(t, 1, g0)
            last.then_inc(w_ready, 1)

            def add(u, s, dst):
                pool.wait_ge(normed, u + 1)
                a = attn[:, s].rearrange("p t j h -> p j t h")
                for j in range(2):
                    ins = nc.gpsimd.tensor_tensor(dst[:, j], dst[:, j], a[:, j], ALU.add)
                ins.then_inc(added, 1)

            def add_cols(u, s, w0):
                add(u, s, image[:, :, 1:H + 1, bass.ds(w0, 2)].rearrange("p t h j -> p j t h"))

            def add_rows(u, s, r0):
                add(u, s, image[:, :, bass.ds(r0 + 1, 2), :].rearrange("p t j w -> p j t w"))

            def lo_parts(before, s):
                for i in range(COMPS):
                    pool.wait_ge(v_hi_done, before + i + 1)
                    nc.gpsimd.tensor_tensor(v_lo[:, s, i, :, :, 1:W + 1], comp[:, i],
                                            v_hi[:, s, i, :, :, 1:W + 1].bitcast(F32), ALU.subtract).then_inc(v_lo_done, 1)

            pool.wait_ge(w_ready, 1)
            pool.wait_ge(summed, 2 * CT * N)
            pool.wait_ge(y_ready, 2 * N)
            for v in (v_hi, v_lo):
                vb = v[:].bitcast(F32).rearrange("p s i t r w -> p (s i t r) w")
                nc.gpsimd.memset(vb[:, :, 0:1], 0.0)
                pads = nc.gpsimd.memset(vb[:, :, WP - 1:WP], 0.0)
            pads.then_inc(v_pads_ready, 1)

            with pool.Fori(0, N) as n:
                u0 = IMG_UNITS * n
                v0 = u0 + DIR_UNITS
                chunks = GROUPS * n
                with pool.Fori(0, GROUPS) as g:
                    for p in range(UPG):
                        u = UPG * g + p
                        add_cols(u0 + u, p % 2, 2 * u)

                def row_group(g, s, lo=True):
                    for p in range(UPG):
                        u = UPG * g + p
                        add_rows(v0 + u, p % 2, 2 * u)
                        if p == 0 and lo:
                            lo_parts(COMPS * (chunks + g - 1), 1 - s)

                pool.wait_ge(added, v0)
                row_group(0, 0, lo=False)
                with pool.Fori(0, GROUPS // 2 - 1) as h:
                    row_group(2 * h + 1, 1)
                    row_group(2 * h + 2, 0)
                row_group(GROUPS - 1, 1)
                lo_parts(COMPS * (chunks + GROUPS - 1), (GROUPS - 1) % 2)

        @block.scalar
        def _(act):
            act.sem_inc(relu_done, FREE)
            act.wait_ge(bn_chain, 1)
            nc.scalar.activation(bn_t[:, 1], bn_t[:, 0], ACT.Sqrt).then_inc(bn_root, 1)

            act.wait_ge(summed, 2 * CT * N)
            for d in range(2):
                for i in range(N):
                    k = d * N + i
                    if k >= 2:
                        act.wait_ge(y_psum, k - 1)
                    nc.scalar.copy(probs[:, k % 2, :, 0:2 * H].rearrange("p t (a h) -> p t a h", a=2),
                                   sums[:, d, :, i].unsqueeze(2).broadcast_to([P, CT, 2, H])).then_inc(sums_twice, 1)

            def copy_hi(u, s, start=False):
                act.wait_ge(xt_done, u + 1)
                if not start:
                    act.wait_ge(scored, 2 * (u - 2) + 2)
                for j in range(2):
                    at = slice(H * j, H * j + H)
                    nc.scalar.copy(xt_sb[at, s, j], xt_ps[at, 0:C]).then_inc(hi_copied, 1)

            def exp(b, j, slot, start=False, slot_free=None):
                act.wait_ge(max_done, b + 1)
                if not start:
                    act.wait_ge(pt_done, b - 1)
                for t in range(CT):
                    if t == CT - 1 and slot_free is not None:
                        act.wait_ge(prod_done, slot_free)
                    ins = nc.scalar.activation(probs[:, j, t], scores[:, j, t], ACT.Exp, bias=neg_max[:, slot, t:t + 1])
                ins.then_inc(exp_done, 1)

            def cols(w0):
                return image[:, :, 1:H + 1, bass.ds(w0, 2)].rearrange("p t h j -> p t j h")

            def rows_of(p, s):
                return rows[:, s, :, 2 * p:2 * p + 2, :]

            def stage(u, p, src):
                nc.scalar.copy(st_x[:, p, :, 1:2 * H + 1].rearrange("p t (j h) -> p t j h", j=2), src).then_inc(staged, 1)

            def copy_pt(u, p, start=False):
                act.wait_ge(pt_done, 2 * u + 1)
                if not start:
                    act.wait_ge(prod_done, u - 1)
                nc.scalar.copy(probs_t[:, 2 * (p % 2)], pt_ps[:, 0]).then_inc(pt_copied[0], 1)

            def unit(u, p, x2, ahead=True, first=False):
                start = first and p == 0
                if ahead:
                    copy_hi(u + 1, (p + 1) % 2, start)
                if not start:
                    copy_pt(u - 1, p - 1, start=first and p < 3)
                exp(2 * u, 0, 2 * (p % 2), start, slot_free=u - UPG + 3 if x2 is not None and not (first and p < 2) else None)
                if x2 is not None:
                    stage(u + 2, (p + 2) % UPG, x2)
                exp(2 * u + 1, 1, 2 * (p % 2) + 1, start)

            def hi_parts(c, s):
                for i in range(COMPS):
                    act.wait_ge(comp_done, COMPS * c + i + 1)
                    nc.scalar.copy(v_hi[:, s, i, :, :, 1:W + 1], comp[:, i]).then_inc(v_hi_done, 1)

            def conv_step(c, q):
                m = q // 2
                if q % 2 == 0:
                    act.wait_ge(conv_done, STEPS * c + q + 1)
                    nc.scalar.copy(m1[:], conv_ps[:, 0, 0]).then_inc(m1_done, 1)
                else:
                    act.wait_ge(conv_taken, CONV_BANKS + STEPS * c + q + 1)
                    act.wait_ge(stored[m], FREE + DMA * c)
                    nc.scalar.activation(out_sb[:, m].rearrange("p (t r) w -> p t r w", r=2), y_rows[:], ACT.Relu,
                                         bias=bn_bias[:, m:m + 1], scale=bn_scale[:, m:m + 1]).then_inc(relu_done, 1)

            act.wait_ge(bn_ready, 1)
            act.wait_ge(v_pads_ready, 1)

            def stage_first(n):
                act.wait_ge(image_in, FREE + DMA * GROUPS * n)
                for p in range(2):
                    stage(IMG_UNITS * n + p, p, cols(2 * p))

            def first_group(n, conv):
                for p in range(UPG):
                    unit(IMG_UNITS * n + p, p, cols(2 * (p + 2)), first=True)
                    if conv:
                        conv_step(GROUPS * n - 1, p)

            def later_groups(n):
                u0 = IMG_UNITS * n
                v0 = u0 + DIR_UNITS
                chunks = GROUPS * n
                loads = GROUPS // 2 * n
                with act.Fori(1, GROUPS - 1) as g:
                    for p in range(UPG):
                        u = UPG * g + p
                        unit(u0 + u, p, cols(2 * (u + 2)))
                for p in range(UPG):
                    u = DIR_UNITS - UPG + p
                    if p == 2:
                        act.wait_ge(rows_in[0], DMA * (loads + 1))
                    unit(u0 + u, p, cols(2 * (u + 2)) if p < 2 else rows_of(p - 2, 0))

                def row_group(g, s, next_loads, conv=True, split=True):
                    last = next_loads is None
                    for p in range(UPG):
                        if p == 2 and not last:
                            act.wait_ge(rows_in[1 - s], DMA * next_loads)
                        x2 = rows_of(p + 2, s) if p < 2 else None if last else rows_of(p - 2, 1 - s)
                        unit(v0 + UPG * g + p, p, x2, ahead=not (last and p == UPG - 1))
                        if p == 2 and split:
                            hi_parts(chunks + g - 1, 1 - s)
                        if conv:
                            conv_step(chunks + g - 2, p)

                row_group(0, 0, loads + 1, conv=False, split=False)
                row_group(1, 1, loads + 2, conv=False)
                with act.Fori(1, GROUPS // 2 - 1) as h:
                    row_group(2 * h, 0, loads + h + 1)
                    row_group(2 * h + 1, 1, loads + h + 2)
                row_group(GROUPS - 2, 0, loads + GROUPS // 2)
                row_group(GROUPS - 1, 1, None)
                copy_pt(u0 + IMG_UNITS - 1, UPG - 1)
                hi_parts(chunks + GROUPS - 1, (GROUPS - 1) % 2)

            stage_first(0)
            copy_hi(0, 0, start=True)
            first_group(0, conv=False)
            with act.Fori(0, N - 1) as n:
                later_groups(n)
                chunk = GROUPS * n + GROUPS - 2
                conv_step(chunk, 0)
                conv_step(chunk, 1)
                stage_first(n + 1)
                conv_step(chunk, 2)
                copy_hi(IMG_UNITS * (n + 1), 0, start=True)
                conv_step(chunk, 3)
                first_group(n + 1, conv=True)
            later_groups(N - 1)
            for c in (GROUPS - 2, GROUPS - 1):
                for q in range(STEPS):
                    conv_step(GROUPS * (N - 1) + c, q)

        @block.vector
        def _(dve):
            dve.wait_ge(small_in, SMALL_LOADS * DMA)
            root, r0, r1, half = (bn_t[:, i] for i in range(1, 5))
            count = [0]

            def link(ins):
                count[0] += 1
                ins.then_inc(bn_chain, 1)
                dve.wait_ge(bn_chain, count[0])

            link(nc.vector.tensor_scalar(bn_t[:, 0], bn[:, 3], BN_EPS, None, ALU.add))
            dve.wait_ge(bn_root, 1)
            link(nc.vector.reciprocal(r0, root))
            link(nc.vector.tensor_tensor(r1, bn_t[:, 0], r0, ALU.mult))
            link(nc.vector.tensor_tensor(half, r1, root, ALU.add))
            link(nc.vector.tensor_scalar(half, half, 0.5, None, ALU.mult))
            link(nc.vector.reciprocal(r0, half))
            link(nc.vector.tensor_tensor(bn_scale[:], bn[:, 0], r0, ALU.mult))
            link(nc.vector.tensor_tensor(r1, bn[:, 2], bn_scale[:], ALU.mult))
            nc.vector.tensor_tensor(bn_bias[:], bn[:, 1], r1, ALU.subtract).then_inc(bn_ready, 1)

            for i in range(N):
                for t in range(CT):
                    dve.wait_ge((sums_in0, sums_in1)[t], DMA * (i + 1))
                    half_image = image[:, t, 1:H + 1, :]
                    nc.vector.tensor_reduce(sums[:, 0, t, N - 1 - i], half_image, AX.X, ALU.add).then_inc(summed, 1)
                    nc.vector.tensor_reduce(sums[:, 1, t, N - 1 - i], half_image.rearrange("p h w -> p w h"),
                                            AX.X, ALU.add).then_inc(summed, 1)

            for d in range(2):
                for i in range(N):
                    k = d * N + i
                    dve.wait_ge(y_psum, k + 1)
                    y = attn[:, k % 2].rearrange("p t j h -> p (t j h)")
                    link(nc.vector.scalar_tensor_tensor(out=y, in0=scores[:, k % 2, 0], scalar=1.0 / W,
                                                        in1=proj_b[:, d], op0=ALU.mult, op1=ALU.add))
                    link(nc.vector.tensor_copy(y_hi[:, d, i], y))
                    nc.vector.tensor_tensor(y_lo[:, d, i], y, y_hi[:, d, i].bitcast(F32), ALU.subtract).then_inc(y_ready, 1)

            def maximum(b, j, slot):
                dve.wait_ge(scored, b + 1)
                nc.vector.tensor_reduce(neg_max[:, slot], scores[:, j], AX.X, ALU.max, negate=True).then_inc(max_done, 1)

            def copy_unit(u, p, j, start=False):
                dve.wait_ge(pt_done, 2 * u + j + 1)
                if not start:
                    dve.wait_ge(prod_done, u - 1)
                nc.vector.tensor_copy(probs_t[:, 2 * (p % 2) + j], pt_ps[:, j]).then_inc(pt_copied[j], 1)

            def norm(u, s, start=False):
                dve.wait_ge(prod_done, u + 1)
                nc.vector.reciprocal(rcp[:, s], prod_v[:, :, 0:2 * H + 2:2 * H + 1]).then_inc(rcp_done, 1)
                if not start:
                    dve.wait_ge(added, u - 1)
                dve.wait_ge(rcp_done, u + 1)
                for j in range(2):
                    ins = nc.vector.scalar_tensor_tensor(out=attn[:, s, :, j], in0=prod_v[:, :, 1 + H * j:1 + H * (j + 1)],
                                                         scalar=gam[:, 0:1], in1=rcp[:, s, :, j:j + 1].broadcast_to([P, CT, H]),
                                                         op0=ALU.mult, op1=ALU.mult)
                ins.then_inc(normed, 1)

            def lo_rows(u, s):
                for j in range(2):
                    dve.wait_ge(hi_copied, 2 * u + j + 1)
                    at, to = slice(H * j, H * j + H), slice(H - H * j, 2 * H - H * j)
                    nc.vector.tensor_tensor(xt_sb[to, s, j], xt_ps[at, 0:C], xt_sb[at, s, j].bitcast(F32),
                                            ALU.subtract).then_inc(xt_ready, 1)

            def unit(u, p, first=False, ahead=True):
                maximum(2 * u, 0, 2 * (p % 2))
                if ahead:
                    lo_rows(u + 1, (p + 1) % 2)
                if not (first and p < 2):
                    norm(u - 2, p % 2, start=first)
                maximum(2 * u + 1, 1, 2 * (p % 2) + 1)
                if not (first and p == 0):
                    copy_unit(u - 1, p - 1, 1, start=first and p < 3)

            def transform(c, r, u, base):
                dve.wait_ge(added, u)
                dve.wait_ge(v_lo_done, FREE + base)
                around = image[:, :, bass.ds(r, ROWS + 2), :]
                d = [around[:, :, i:i + ROWS - 1:2, :] for i in range(4)]
                for i, (a, b, op) in enumerate(((0, 2, ALU.subtract), (1, 2, ALU.add), (2, 1, ALU.subtract), (1, 3, ALU.subtract))):
                    nc.vector.tensor_tensor(comp[:, i], d[a], d[b], op).then_inc(comp_done, 1)

            def conv_step(c, q):
                m, k = q // 2, STEPS * c + q
                if q % 2 == 0:
                    dve.wait_ge(m1_done, CT * c + m + 1)
                    nc.vector.tensor_tensor(m12_sum[:], conv_ps[:, 0, 1], m1[:], ALU.add)
                    nc.vector.tensor_tensor(m12_dif[:], m1[:], conv_ps[:, 0, 1], ALU.subtract).then_inc(conv_taken, 1)
                else:
                    dve.wait_ge(conv_done, k + 1)
                    dve.wait_ge(conv_taken, CONV_BANKS + k)
                    dve.wait_ge(relu_done, FREE + CT * c + m)
                    nc.vector.tensor_tensor(y_rows[:, :, 0], conv_ps[:, 1, 0], m12_sum[:], ALU.add)
                    nc.vector.tensor_tensor(y_rows[:, :, 1], m12_dif[:], conv_ps[:, 1, 1], ALU.subtract).then_inc(conv_taken, 1)

            dve.sem_inc(conv_taken, CONV_BANKS)
            dve.wait_ge(pads_ready, 1)

            def first_group(n, conv):
                for p in range(UPG):
                    unit(IMG_UNITS * n + p, p, first=True)
                    if conv:
                        conv_step(GROUPS * n - 1, p)

            def later_groups(n):
                u0 = IMG_UNITS * n
                v0 = u0 + DIR_UNITS
                chunks = GROUPS * n

                def transform_chunk(g):
                    transform(chunks + g, ROWS * g, v0 + UPG * (g + 1) + 1, COMPS * (chunks + g))

                with dve.Fori(1, GROUPS + 1) as g:
                    for p in range(UPG):
                        unit(u0 + UPG * g + p, p)
                for p in range(UPG):
                    unit(v0 + UPG + p, p)
                    if p == 2:
                        transform_chunk(0)

                def row_group(g, last=False):
                    for p in range(UPG):
                        unit(v0 + UPG * g + p, p, ahead=not (last and p == UPG - 1))
                        if p == 2:
                            transform_chunk(g - 1)
                        conv_step(chunks + g - 2, p)

                with dve.Fori(2, GROUPS - 1) as g:
                    row_group(g)
                row_group(GROUPS - 1, last=True)
                last = u0 + IMG_UNITS - 1
                norm(last - 1, 0)
                copy_unit(last, UPG - 1, 1)
                norm(last, 1)
                transform(chunks + GROUPS - 1, ROWS * (GROUPS - 1), last + 1, COMPS * (chunks + GROUPS - 1))

            lo_rows(0, 0)
            first_group(0, conv=False)
            with dve.Fori(0, N - 1) as n:
                later_groups(n)
                for q in range(STEPS):
                    if q == STEPS - 1:
                        lo_rows(IMG_UNITS * (n + 1), 0)
                    conv_step(GROUPS * n + GROUPS - 2, q)
                first_group(n + 1, conv=True)
            later_groups(N - 1)
            for c in (GROUPS - 2, GROUPS - 1):
                for q in range(STEPS):
                    conv_step(GROUPS * (N - 1) + c, q)

        @block.tensor
        def _(pe):
            pe.wait_ge(small_in, SMALL_LOADS * DMA)
            for d in range(2):
                for i in range(N):
                    k = d * N + i
                    pe.wait_ge(sums_twice, k + 1)
                    if k >= 2:
                        pe.wait_ge(y_ready, k - 1)
                    for t in range(CT):
                        ins = nc.tensor.matmul(scores[:, k % 2, 0], probs[:, k % 2, t, 0:2 * H], proj[:, d, t], start=t == 0, stop=t == CT - 1)
                    ins.then_inc(y_psum, 1)
            pe.wait_ge(ident_ready, 1)
            pe.wait_ge(ones_ready, 1)
            pe.wait_ge(w_ready, 1)
            pe.wait_ge(y_ready, 2 * N)

            def transpose_x(u, p, start=False):
                pe.wait_ge(staged, u + 1)
                if not start:
                    pe.wait_ge(xt_ready, 2 * u)
                for t in range(CT):
                    ins = nc.tensor.transpose(xt_ps[:, t * P:(t + 1) * P], st_x[:, p, t, 1:2 * H + 1], ident[:])
                ins.then_inc(xt_done, 1)

            def score(u, p, j, d, start=False):
                pe.wait_ge(xt_ready, 2 * u + j + 1)
                if not start:
                    pe.wait_ge(exp_done, 2 * u + j - 1)
                for t in range(CT):
                    for y, flag in ((y_hi, True), (y_lo, False)):
                        ins = nc.tensor.matmul(scores[:, j, t], xt_sb[:, p % 2, j, t * P:(t + 1) * P],
                                               y[:, d, 2 * p + j], start=flag, stop=not flag)
                ins.then_inc(scored, 1)

            def transpose_p(u, j, start=False):
                pe.wait_ge(exp_done, 2 * u + j + 1)
                if not start:
                    pe.wait_ge(pt_copied[j], u)
                for t in range(CT):
                    for k in range(CT):
                        ins = nc.tensor.transpose(pt_ps[:, j, k, t * P:(t + 1) * P],
                                                  probs[:, j, t, k * P:(k + 1) * P], ident[:])
                ins.then_inc(pt_done, 1)

            def product(u, p, start=False):
                if not start:
                    pe.wait_ge(normed, u)
                for j in range(2):
                    pe.wait_ge(pt_copied[j], u + 1)
                    for t in range(CT):
                        for k in range(CT):
                            half = slice((H + 1) * j, (H + 1) * (j + 1))
                            ins = nc.tensor.matmul(prod_v[:, t, half], probs_t[:, 2 * (p % 2) + j, k, t * P:(t + 1) * P],
                                                   st_x[:, p, k, half], start=k == 0, stop=k == CT - 1)
                ins.then_inc(prod_done, 1)

            def unit(u, p, d, first=False, ahead=True):
                start, before = first and p == 0, not (first and p == 0)
                score(u, p, 0, d, start)
                if before:
                    transpose_p(u - 1, 0, start=first and p == 1)
                if ahead:
                    transpose_x(u + 1, (p + 1) % UPG)
                if not (first and p < 2):
                    product(u - 2, (p - 2) % UPG, start=first and p == 2)
                score(u, p, 1, d, start)
                if before:
                    transpose_p(u - 1, 1, start=first and p == 1)

            def conv_step(c, q, s):
                m, half, k = q // 2, q % 2, STEPS * c + q
                if q == 0:
                    pe.wait_ge(v_lo_done, FREE + COMPS * (c + 1))
                pe.wait_ge(conv_taken, CONV_BANKS + k - 1)
                for b, i in enumerate(STEP_COMPS[half]):
                    parts = [(t, kw, w, v) for t in range(CT) for kw in range(KW)
                             for w, v in ((w_hi, v_hi), (w_hi, v_lo), (w_lo, v_hi))]
                    for a, (t, kw, w, v) in enumerate(parts):
                        ins = nc.tensor.matmul(conv_ps[:, half, b], w[:, t, i, kw, m * P:(m + 1) * P],
                                               v[:, s, i, t, :, kw:kw + W], start=a == 0, stop=a == len(parts) - 1)
                ins.then_inc(conv_done, 1)


            def first_group(n, conv):
                for p in range(UPG):
                    unit(IMG_UNITS * n + p, p, 0, first=True)
                    if conv:
                        conv_step(GROUPS * n - 1, p, (GROUPS - 1) % 2)

            def later_groups(n):
                u0 = IMG_UNITS * n
                v0 = u0 + DIR_UNITS
                chunks = GROUPS * n
                with pe.Fori(1, GROUPS) as g:
                    for p in range(UPG):
                        unit(u0 + UPG * g + p, p, 0)
                with pe.Fori(0, 2) as g:
                    for p in range(UPG):
                        unit(v0 + UPG * g + p, p, 1)

                def row_group(g, s, last=False):
                    for p in range(UPG):
                        unit(v0 + UPG * g + p, p, 1, ahead=not (last and p == UPG - 1))
                        conv_step(chunks + g - 2, p, s)

                with pe.Fori(1, GROUPS // 2 - 1) as h:
                    row_group(2 * h, 0)
                    row_group(2 * h + 1, 1)
                row_group(GROUPS - 2, 0)
                row_group(GROUPS - 1, 1, last=True)
                last = u0 + IMG_UNITS - 1
                product(last - 1, UPG - 2)
                transpose_p(last, 0)
                transpose_p(last, 1)
                product(last, UPG - 1)

            transpose_x(0, 0, start=True)
            first_group(0, conv=False)
            with pe.Fori(0, N - 1) as n:
                later_groups(n)
                for q in range(STEPS):
                    if q == STEPS - 1:
                        transpose_x(IMG_UNITS * (n + 1), 0, start=True)
                    conv_step(GROUPS * n + GROUPS - 2, q, 0)
                first_group(n + 1, conv=True)
            later_groups(N - 1)
            for c in (GROUPS - 2, GROUPS - 1):
                for q in range(STEPS):
                    conv_step(GROUPS * (N - 1) + c, q, c % 2)


def kernel(x, L0_conv_wh, L0_conv_bh, L0_conv_ww, L0_conv_bw, L0_conv_conv_k, L0_conv_bn_w, L0_conv_bn_b,
           L0_conv_bn_mean, L0_conv_bn_var, L0_conv_gamma):
    import concourse.bacc as bacc
    import numpy as np
    from concourse.bass_utils import run_bass_kernel_spmd

    arrays = {
        "x": np.ascontiguousarray(x),
        "wh_t": np.ascontiguousarray(np.asarray(L0_conv_wh).T),
        "bh": np.ascontiguousarray(L0_conv_bh),
        "ww_t": np.ascontiguousarray(np.asarray(L0_conv_ww).T),
        "bw": np.ascontiguousarray(L0_conv_bw),
        "conv_t": np.ascontiguousarray(np.asarray(L0_conv_conv_k).transpose(1, 2, 3, 0)).reshape(C, 3, KW * C),
        "bn_params": np.ascontiguousarray(np.stack([L0_conv_bn_w, L0_conv_bn_b, L0_conv_bn_mean, L0_conv_bn_var])
                                          .reshape(4, CT, P).transpose(2, 0, 1)),
        "gamma": np.ascontiguousarray(L0_conv_gamma),
    }
    nc = bacc.Bacc("TRN2", target_bir_lowering=False, num_devices=1)
    aps = {name: nc.dram_tensor(name, a.shape, mybir.dt.from_np(a.dtype), kind="ExternalInput").ap()
           for name, a in arrays.items()}
    out = nc.dram_tensor("out", (N, C, H, W), F32, kind="ExternalOutput").ap()
    build(nc, **aps, out=out)
    result = run_bass_kernel_spmd(nc, [arrays], core_ids=[0])
    return result.results[0]["out"]
```

```python
from contextlib import ExitStack

import concourse.bass as bass
from concourse import mybir

F32 = mybir.dt.float32
F32R = mybir.dt.float32r
ALU = mybir.AluOpType
ACT = mybir.ActivationFunctionType
AX = mybir.AxisListType

P = 128
N, C, H, W = 8, 256, 64, 64
CT = C // P
UPG = 4
ROWS = 2 * UPG
GROUPS = H // ROWS
DIR_UNITS = UPG * GROUPS
IMG_UNITS = 2 * DIR_UNITS
QUARTERS = 4
COMPS = 4
KW = 3
PAIRS = ROWS // 2
WP = W + 2
STEPS = 4
IMG_STEPS = STEPS * GROUPS
DMA = 16
CONV_BANKS = 2
FREE = 1
SMALL_LOADS = 6
BN_EPS = 1e-5
STEP_COMPS = ((1, 2), (0, 3))


def build(nc, x, wh_t, bh, ww_t, bw, conv_t, bn_params, gamma, out):
    ctx = ExitStack()
    with ctx:
        def sb(name, shape, dt=F32, stack=ctx):
            return stack.enter_context(nc.sbuf_tensor(name, shape, dt))

        def sem(name):
            return ctx.enter_context(nc.semaphore(name))

        image = sb("image", [P, CT, H + 2, W])
        rows = sb("rows", [P, 2, CT, ROWS, W])
        y_hi = sb("y_hi", [P, 2, N, C], F32R)
        y_lo = sb("y_lo", [P, 2, N, C], F32R)
        w_hi = sb("w_hi", [P, CT, COMPS, KW, C], F32R)
        w_lo = sb("w_lo", [P, CT, COMPS, KW, C], F32R)
        st_x = sb("st_x", [P, UPG, CT, 2 * H + 2])
        xt_sb = sb("xt_sb", [P, 2, 2, C], F32R)
        probs = sb("probs", [P, 2, CT, C])
        probs_t = sb("probs_t", [P, 4, CT, C])
        neg_max = sb("neg_max", [P, 4, CT])
        rcp = sb("rcp", [P, 2, CT, 2])
        attn = sb("attn", [P, 2, CT, 2, H])
        comp = sb("comp", [P, COMPS, CT, PAIRS, W])
        m1 = sb("m1", [P, PAIRS, W])
        m12_sum = sb("m12_sum", [P, PAIRS, W])
        m12_dif = sb("m12_dif", [P, PAIRS, W])
        y_rows = sb("y_rows", [P, PAIRS, 2, W])
        out_sb = sb("out_sb", [P, CT, ROWS, W])
        ident = sb("ident", [P, P])
        gam = sb("gam", [P, 1])
        bn = sb("bn", [P, 4, CT])
        bn_t = sb("bn_t", [P, 6, CT])
        bn_scale = sb("bn_scale", [P, CT])
        bn_bias = sb("bn_bias", [P, CT])
        with ExitStack() as early:
            conv_raw = sb("conv_raw", [P, CT, 3, KW * C], stack=early)
            proj = sb("proj", [P, 2, CT, C], stack=early)
            proj_b = sb("proj_b", [1, 2, C], stack=early)
            ones_row = sb("ones_row", [1, P], stack=early)
            quarter_cols = sb("quarter_cols", [P, W], stack=early)
            folded = sb("folded", [P, W], stack=early)
            sums = sb("sums", [P, 2, CT, N, H], stack=early)
        v_hi = sb("v_hi", [P, 2, COMPS, CT, PAIRS, WP], F32R)
        v_lo = sb("v_lo", [P, 2, COMPS, CT, PAIRS, WP], F32R)

        def ps(name, shape):
            return ctx.enter_context(nc.psum_tensor(name, shape, F32))

        xt_ps = ps("xt_ps", [P, 512])
        scores = ps("scores", [P, 2, CT, C])
        pt_ps = ps("pt_ps", [P, 2, CT, C])
        prod = ps("prod", [P, 512])
        conv_ps = ps("conv_ps", [P, 2, 2, PAIRS, W])
        prod_v = prod[:, 0:CT * (2 * H + 2)].rearrange("p (t c) -> p t c", t=CT)

        weights_in, small_in = sem("weights_in"), sem("small_in")
        sums_in = [sem(f"sums_in{q}") for q in range(QUARTERS)]
        image_in = sem("image_in")
        rows_in = [sem("rows_in0"), sem("rows_in1")]
        ident_ready, pads_ready, ones_ready = sem("ident_ready"), sem("pads_ready"), sem("ones_ready")
        rows_summed, cols_read, cols_summed = sem("rows_summed"), sem("cols_read"), sem("cols_summed")
        last_quarter_summed, folded_done = sem("last_quarter_summed"), sem("folded_done")
        sums_twice, y_psum, y_hi_done, y_ready = sem("sums_twice"), sem("y_psum"), sem("y_hi_done"), sem("y_ready")
        w_chain, w_ready = sem("w_chain"), sem("w_ready")
        bn_chain, bn_root, bn_ready = sem("bn_chain"), sem("bn_root"), sem("bn_ready")
        v_pads_ready = sem("v_pads_ready")
        staged, xt_done, hi_copied, xt_ready = sem("staged"), sem("xt_done"), sem("hi_copied"), sem("xt_ready")
        scored, max_done, exp_done = sem("scored"), sem("max_done"), sem("exp_done")
        pt_done = sem("pt_done")
        pt_copied = [sem("pt_copied0"), sem("pt_copied1")]
        prod_done, rcp_done, normed, added = sem("prod_done"), sem("rcp_done"), sem("normed"), sem("added")
        comp_done, v_hi_done, v_lo_done = sem("comp_done"), sem("v_hi_done"), sem("v_lo_done")
        conv_done, m1_done, half_done, conv_taken = sem("conv_done"), sem("m1_done"), sem("half_done"), sem("conv_taken")
        relu_done = sem("relu_done")
        stored = [sem("stored0"), sem("stored1")]

        def quarter(q):
            return image[:, q // 2, 1 + H // 2 * (q % 2):1 + H // 2 * (q % 2 + 1), :]

        def by_tile(ap):
            return ap.rearrange("(t p) h w -> p t h w", p=P)

        block = ctx.enter_context(nc.Block())

        @block.sync
        def _(sp):
            for s in (image_in, *stored):
                sp.sem_inc(s, FREE)

            def sum_load(i):
                for q in range(QUARTERS):
                    if i:
                        sp.wait_ge(rows_summed, QUARTERS * (i - 1) + q + 1)
                        if q < QUARTERS - 1:
                            sp.wait_ge(cols_read, (QUARTERS - 1) * (i - 1) + q + 1)
                        else:
                            sp.wait_ge(last_quarter_summed, i)
                    sp.dma_start(quarter(q), x[N - 1 - i][P * (q // 2):P * (q // 2 + 1), H // 2 * (q % 2):H // 2 * (q % 2 + 1), :]) \
                        .then_inc(sums_in[q], DMA)

            sum_load(0)
            for d, w_ap in enumerate((wh_t, ww_t)):
                sp.dma_start(proj[:, d], w_ap.rearrange("(t p) c -> p t c", p=P)).then_inc(small_in, DMA)
            for d, b_ap in enumerate((bh, bw)):
                sp.dma_start(proj_b[:, d], b_ap.unsqueeze(0)).then_inc(small_in, DMA)
            sp.dma_start(bn[:], bn_params).then_inc(small_in, DMA)
            sp.dma_start(gam[:], gamma.partition_broadcast(P)).then_inc(small_in, DMA)
            sp.dma_start(conv_raw[:], conv_t.rearrange("(t p) kh m -> p t kh m", p=P)).then_inc(weights_in, DMA)
            for i in range(1, N):
                sum_load(i)

            def load_rows(n, g):
                sp.dma_start(rows[:, g % 2], by_tile(x[n])[:, :, ROWS * g:ROWS * g + ROWS, :]).then_inc(rows_in[g % 2], DMA)

            def one_image(n, last):
                for g in range(2):
                    if not (isinstance(n, int) and n == 0):
                        sp.wait_ge(staged, IMG_UNITS * n)
                    load_rows(n, g)
                for g in range(GROUPS + 2):
                    if g + 2 < GROUPS:
                        sp.wait_ge(staged, IMG_UNITS * n + DIR_UNITS + UPG * (g + 1))
                        load_rows(n, g + 2)
                    loads = [g - 2] if 2 <= g < GROUPS else [GROUPS - 2, GROUPS - 1] if g == GROUPS else []
                    if loads and not last:
                        c = min(g - 1, GROUPS - 1)
                        sp.wait_ge(comp_done, COMPS * (GROUPS * n + c + 1))
                        for k in loads:
                            sp.dma_start(image[:, :, 1 + ROWS * k:1 + ROWS * (k + 1), :],
                                         by_tile(x[n + 1])[:, :, ROWS * k:ROWS * (k + 1), :]).then_inc(image_in, DMA)
                    if g >= 2:
                        for m in range(CT):
                            sp.wait_ge(relu_done, FREE + CT * (GROUPS * n + g - 2) + m + 1)
                            sp.dma_start(by_tile(out[n])[:, m, ROWS * (g - 2):ROWS * (g - 1), :], out_sb[:, m]) \
                                .then_inc(stored[m], DMA)

            one_image(0, False)
            with sp.Fori(1, N - 1) as n:
                one_image(n, False)
            one_image(N - 1, True)
            for m in range(CT):
                sp.wait_ge(stored[m], FREE + DMA * N * GROUPS)

        @block.gpsimd
        def _(pool):
            pool.sem_inc(v_lo_done, FREE)
            nc.gpsimd.memset(ident[:], 0.0).then_inc(w_chain, 1)
            pool.wait_ge(w_chain, 1)
            nc.gpsimd.affine_select(out=ident[:], in_=ident[:], compare_op=ALU.not_equal, fill=1.0, base=0,
                                    pattern=[[-1, P]], channel_multiplier=1).then_inc(ident_ready, 1)
            nc.gpsimd.memset(ones_row[:], 1.0)
            nc.gpsimd.memset(image[:, :, 0, :], 0.0)
            nc.gpsimd.memset(image[:, :, H + 1, :], 0.0).then_inc(pads_ready, 1)
            ones = nc.gpsimd.memset(st_x[:].rearrange("p u t c -> p (u t) c")[:, :, 0:2 * H + 2:2 * H + 1], 1.0)
            ones.then_inc(ones_ready, 1)

            pool.wait_ge(weights_in, DMA)
            count = [1]

            def link(ins):
                count[0] += 1
                ins.then_inc(w_chain, 1)
                pool.wait_ge(w_chain, count[0])

            def split_weights(t, c, w):
                hi, lo = (a[:, t, c].rearrange("p k c -> p (k c)") for a in (w_hi, w_lo))
                link(nc.gpsimd.tensor_scalar(hi, w, 1.0, 0.0, ALU.mult, ALU.add))
                return nc.gpsimd.tensor_tensor(lo, w, hi.bitcast(F32), ALU.subtract)

            for t in range(CT):
                g0, g1, g2 = (conv_raw[:, t, k] for k in range(3))
                split_weights(t, 0, g0)
                link(split_weights(t, 3, g2))
                link(nc.gpsimd.tensor_tensor(g0, g0, g2, ALU.add))
                link(nc.gpsimd.tensor_scalar(g0, g0, 0.5, 0.0, ALU.mult, ALU.add))
                link(nc.gpsimd.tensor_scalar(g1, g1, 0.5, 0.0, ALU.mult, ALU.add))
                link(nc.gpsimd.tensor_tensor(g2, g0, g1, ALU.subtract))
                split_weights(t, 2, g2)
                link(nc.gpsimd.tensor_tensor(g0, g0, g1, ALU.add))
                last = split_weights(t, 1, g0)
            last.then_inc(w_ready, 1)

            def add(u, s, dst):
                pool.wait_ge(normed, u + 1)
                a = attn[:, s].rearrange("p t j h -> p j t h")
                for j in range(2):
                    ins = nc.gpsimd.tensor_tensor(dst[:, j], dst[:, j], a[:, j], ALU.add)
                ins.then_inc(added, 1)

            def add_cols(u, s, w0):
                add(u, s, image[:, :, 1:H + 1, bass.ds(w0, 2)].rearrange("p t h j -> p j t h"))

            def add_rows(u, s, r0):
                add(u, s, image[:, :, bass.ds(r0 + 1, 2), :].rearrange("p t j w -> p j t w"))

            def lo_parts(before, s):
                for i in range(COMPS):
                    pool.wait_ge(v_hi_done, before + i + 1)
                    nc.gpsimd.tensor_tensor(v_lo[:, s, i, :, :, 1:W + 1], comp[:, i],
                                            v_hi[:, s, i, :, :, 1:W + 1].bitcast(F32), ALU.subtract).then_inc(v_lo_done, 1)

            pool.wait_ge(w_ready, 1)
            pool.wait_ge(y_ready, 2 * N)
            for v in (v_hi, v_lo):
                vb = v[:].bitcast(F32).rearrange("p s i t r w -> p (s i t r) w")
                nc.gpsimd.memset(vb[:, :, 0:1], 0.0)
                pads = nc.gpsimd.memset(vb[:, :, WP - 1:WP], 0.0)
            pads.then_inc(v_pads_ready, 1)

            with pool.Fori(0, N) as n:
                u0 = IMG_UNITS * n
                v0 = u0 + DIR_UNITS
                chunks = GROUPS * n
                with pool.Fori(0, GROUPS) as g:
                    for p in range(UPG):
                        u = UPG * g + p
                        add_cols(u0 + u, p % 2, 2 * u)

                def row_group(g, s, lo=True):
                    for p in range(UPG):
                        u = UPG * g + p
                        add_rows(v0 + u, p % 2, 2 * u)
                        if p == 0 and lo:
                            lo_parts(COMPS * (chunks + g - 1), 1 - s)

                pool.wait_ge(added, v0)
                row_group(0, 0, lo=False)
                with pool.Fori(0, GROUPS // 2 - 1) as h:
                    row_group(2 * h + 1, 1)
                    row_group(2 * h + 2, 0)
                row_group(GROUPS - 1, 1)
                lo_parts(COMPS * (chunks + GROUPS - 1), (GROUPS - 1) % 2)

        @block.scalar
        def _(act):
            act.sem_inc(relu_done, FREE)
            act.wait_ge(bn_chain, 1)
            nc.scalar.activation(bn_t[:, 1], bn_t[:, 0], ACT.Sqrt).then_inc(bn_root, 1)

            for i in range(N):
                n = N - 1 - i
                act.wait_ge(cols_summed, CT * (i + 1))
                for d in range(2):
                    if i:
                        act.wait_ge(y_psum, 2 * (i - 1) + d + 1)
                    nc.scalar.activation(probs[:, d, :, 0:2 * H].rearrange("p t (a h) -> p t a h", a=2),
                                         sums[:, d, :, n].unsqueeze(2).broadcast_to([P, CT, 2, H]),
                                         ACT.Copy, scale=1.0 / W).then_inc(sums_twice, 1)
                for d in range(2):
                    act.wait_ge(y_psum, 2 * i + d + 1)
                    nc.scalar.copy(y_hi[:, d, n], scores[:, d, 0]).then_inc(y_hi_done, 1)

            def copy_hi(u, s, start=False):
                act.wait_ge(xt_done, u + 1)
                if not start:
                    act.wait_ge(scored, 2 * (u - 2) + 2)
                for j in range(2):
                    at = slice(H * j, H * j + H)
                    nc.scalar.copy(xt_sb[at, s, j], xt_ps[at, 0:C]).then_inc(hi_copied, 1)

            def exp(b, j, slot, start=False, slot_free=None):
                act.wait_ge(max_done, b + 1)
                if not start:
                    act.wait_ge(pt_done, b - 1)
                for t in range(CT):
                    if t == CT - 1 and slot_free is not None:
                        act.wait_ge(prod_done, slot_free)
                    ins = nc.scalar.activation(probs[:, j, t], scores[:, j, t], ACT.Exp, bias=neg_max[:, slot, t:t + 1])
                ins.then_inc(exp_done, 1)

            def cols(w0):
                return image[:, :, 1:H + 1, bass.ds(w0, 2)].rearrange("p t h j -> p t j h")

            def rows_of(p, s):
                return rows[:, s, :, 2 * p:2 * p + 2, :]

            def stage(u, p, src):
                nc.scalar.copy(st_x[:, p, :, 1:2 * H + 1].rearrange("p t (j h) -> p t j h", j=2), src).then_inc(staged, 1)

            def copy_pt(u, p, start=False):
                act.wait_ge(pt_done, 2 * u + 1)
                if not start:
                    act.wait_ge(prod_done, u - 1)
                nc.scalar.copy(probs_t[:, 2 * (p % 2)], pt_ps[:, 0]).then_inc(pt_copied[0], 1)

            def unit(u, p, x2, ahead=True, first=False):
                start = first and p == 0
                if ahead:
                    copy_hi(u + 1, (p + 1) % 2, start)
                if not start:
                    copy_pt(u - 1, p - 1, start=first and p < 3)
                restage = x2 is not None and not (first and p < 2)
                exp(2 * u, 0, 2 * (p % 2), start, slot_free=u - UPG + 3 if restage else None)
                if x2 is not None:
                    stage(u + 2, (p + 2) % UPG, x2)
                exp(2 * u + 1, 1, 2 * (p % 2) + 1, start)

            def hi_parts(c, s):
                for i in range(COMPS):
                    act.wait_ge(comp_done, COMPS * c + i + 1)
                    nc.scalar.copy(v_hi[:, s, i, :, :, 1:W + 1], comp[:, i]).then_inc(v_hi_done, 1)

            def conv_step(c, q):
                m = q // 2
                if q % 2 == 0:
                    act.wait_ge(conv_done, STEPS * c + q + 1)
                    nc.scalar.copy(m1[:], conv_ps[:, 0, 0]).then_inc(m1_done, 1)
                else:
                    act.wait_ge(conv_taken, CONV_BANKS + STEPS * c + q + 1)
                    act.wait_ge(stored[m], FREE + DMA * c)
                    nc.scalar.activation(out_sb[:, m].rearrange("p (t r) w -> p t r w", r=2), y_rows[:], ACT.Relu,
                                         bias=bn_bias[:, m:m + 1], scale=bn_scale[:, m:m + 1]).then_inc(relu_done, 1)

            act.wait_ge(bn_ready, 1)
            act.wait_ge(v_pads_ready, 1)

            def stage_first(n):
                act.wait_ge(image_in, FREE + DMA * GROUPS * n)
                for p in range(2):
                    stage(IMG_UNITS * n + p, p, cols(2 * p))

            def first_group(n, conv):
                for p in range(UPG):
                    unit(IMG_UNITS * n + p, p, cols(2 * (p + 2)), first=True)
                    if conv:
                        conv_step(GROUPS * n - 1, p)

            def later_groups(n):
                u0 = IMG_UNITS * n
                v0 = u0 + DIR_UNITS
                chunks = GROUPS * n
                loads = GROUPS // 2 * n
                with act.Fori(1, GROUPS - 1) as g:
                    for p in range(UPG):
                        u = UPG * g + p
                        unit(u0 + u, p, cols(2 * (u + 2)))
                for p in range(UPG):
                    u = DIR_UNITS - UPG + p
                    if p == 2:
                        act.wait_ge(rows_in[0], DMA * (loads + 1))
                    unit(u0 + u, p, cols(2 * (u + 2)) if p < 2 else rows_of(p - 2, 0))

                def row_group(g, s, next_loads, conv=True, split=True):
                    last = next_loads is None
                    for p in range(UPG):
                        if p == 2 and not last:
                            act.wait_ge(rows_in[1 - s], DMA * next_loads)
                        x2 = rows_of(p + 2, s) if p < 2 else None if last else rows_of(p - 2, 1 - s)
                        unit(v0 + UPG * g + p, p, x2, ahead=not (last and p == UPG - 1))
                        if p == 2 and split:
                            hi_parts(chunks + g - 1, 1 - s)
                        if conv:
                            conv_step(chunks + g - 2, p)

                row_group(0, 0, loads + 1, conv=False, split=False)
                row_group(1, 1, loads + 2, conv=False)
                with act.Fori(1, GROUPS // 2 - 1) as h:
                    row_group(2 * h, 0, loads + h + 1)
                    row_group(2 * h + 1, 1, loads + h + 2)
                row_group(GROUPS - 2, 0, loads + GROUPS // 2)
                row_group(GROUPS - 1, 1, None)
                copy_pt(u0 + IMG_UNITS - 1, UPG - 1)
                hi_parts(chunks + GROUPS - 1, (GROUPS - 1) % 2)

            stage_first(0)
            copy_hi(0, 0, start=True)
            first_group(0, conv=False)
            with act.Fori(0, N - 1) as n:
                later_groups(n)
                chunk = GROUPS * n + GROUPS - 2
                conv_step(chunk, 0)
                conv_step(chunk, 1)
                stage_first(n + 1)
                conv_step(chunk, 2)
                copy_hi(IMG_UNITS * (n + 1), 0, start=True)
                conv_step(chunk, 3)
                first_group(n + 1, conv=True)
            later_groups(N - 1)
            for c in (GROUPS - 2, GROUPS - 1):
                for q in range(STEPS):
                    conv_step(GROUPS * (N - 1) + c, q)

        @block.vector
        def _(dve):
            root, r0, r1, mean_root = (bn_t[:, i] for i in range(1, 5))
            count = [0]

            def link(ins):
                count[0] += 1
                ins.then_inc(bn_chain, 1)
                dve.wait_ge(bn_chain, count[0])

            def norm_constants():
                dve.wait_ge(small_in, SMALL_LOADS * DMA)
                link(nc.vector.tensor_scalar(bn_t[:, 0], bn[:, 3], BN_EPS, None, ALU.add))
                dve.wait_ge(bn_root, 1)
                link(nc.vector.reciprocal(r0, root))
                link(nc.vector.tensor_tensor(r1, bn_t[:, 0], r0, ALU.mult))
                link(nc.vector.tensor_tensor(mean_root, r1, root, ALU.add))
                link(nc.vector.tensor_scalar(mean_root, mean_root, 0.5, None, ALU.mult))
                link(nc.vector.reciprocal(r0, mean_root))
                link(nc.vector.tensor_tensor(bn_scale[:], bn[:, 0], r0, ALU.mult))
                link(nc.vector.tensor_tensor(r1, bn[:, 2], bn_scale[:], ALU.mult))
                nc.vector.tensor_tensor(bn_bias[:], bn[:, 1], r1, ALU.subtract).then_inc(bn_ready, 1)

            def cols_fold(k):
                i, t = k // CT, k % CT
                dve.wait_ge(cols_read, (QUARTERS - 1) * i + 2 + t)
                partial = pt_ps[:, t].rearrange("p t (r w) -> p w (t r)", w=W)
                if t == 0:
                    nc.vector.tensor_reduce(sums[:, 1, t, N - 1 - i], partial, AX.X, ALU.add).then_inc(cols_summed, 1)
                else:
                    nc.vector.tensor_reduce(folded[:], partial, AX.X, ALU.add).then_inc(folded_done, 1)
                    dve.wait_ge(folded_done, i + 1)
                    dve.wait_ge(last_quarter_summed, i + 1)
                    nc.vector.tensor_tensor(sums[:, 1, t, N - 1 - i], folded[:], quarter_cols[:], ALU.add).then_inc(cols_summed, 1)

            def tables_lo(i):
                for d in range(2):
                    dve.wait_ge(y_hi_done, 2 * i + d + 1)
                    nc.vector.tensor_tensor(y_lo[:, d, N - 1 - i], scores[:, d, 0], y_hi[:, d, N - 1 - i].bitcast(F32),
                                            ALU.subtract).then_inc(y_ready, 1)

            for k in range(CT * N):
                for a in range(2):
                    q = 2 * (k % CT) + a
                    rows_of_q = slice(H // 2 * a, H // 2 * (a + 1))
                    dve.wait_ge(sums_in[q], DMA * (k // CT + 1))
                    nc.vector.tensor_reduce(sums[:, 0, k % CT, N - 1 - k // CT, rows_of_q], quarter(q), AX.X, ALU.add) \
                        .then_inc(rows_summed, 1)
                    if q == QUARTERS - 1:
                        if k >= CT:
                            dve.wait_ge(cols_summed, k - 1)
                        nc.vector.tensor_reduce(quarter_cols[:], quarter(q).rearrange("p h w -> p w h"), AX.X, ALU.add) \
                            .then_inc(last_quarter_summed, 1)
                if k:
                    cols_fold(k - 1)
                if k % CT == 0 and k >= 2 * CT:
                    tables_lo(k // CT - 2)
                if k == 2 * CT - 1:
                    norm_constants()
            cols_fold(CT * N - 1)
            tables_lo(N - 2)
            tables_lo(N - 1)

            def maximum(b, j, slot):
                dve.wait_ge(scored, b + 1)
                nc.vector.tensor_reduce(neg_max[:, slot], scores[:, j], AX.X, ALU.max, negate=True).then_inc(max_done, 1)

            def copy_unit(u, p, j, start=False):
                dve.wait_ge(pt_done, 2 * u + j + 1)
                if not start:
                    dve.wait_ge(prod_done, u - 1)
                nc.vector.tensor_copy(probs_t[:, 2 * (p % 2) + j], pt_ps[:, j]).then_inc(pt_copied[j], 1)

            def norm(u, s, start=False):
                dve.wait_ge(prod_done, u + 1)
                nc.vector.reciprocal(rcp[:, s], prod_v[:, :, 0:2 * H + 2:2 * H + 1]).then_inc(rcp_done, 1)
                if not start:
                    dve.wait_ge(added, u - 1)
                dve.wait_ge(rcp_done, u + 1)
                for j in range(2):
                    ins = nc.vector.scalar_tensor_tensor(out=attn[:, s, :, j], in0=prod_v[:, :, 1 + H * j:1 + H * (j + 1)],
                                                         scalar=gam[:, 0:1], in1=rcp[:, s, :, j:j + 1].broadcast_to([P, CT, H]),
                                                         op0=ALU.mult, op1=ALU.mult)
                ins.then_inc(normed, 1)

            def lo_rows(u, s):
                for j in range(2):
                    dve.wait_ge(hi_copied, 2 * u + j + 1)
                    at, to = slice(H * j, H * j + H), slice(H - H * j, 2 * H - H * j)
                    nc.vector.tensor_tensor(xt_sb[to, s, j], xt_ps[at, 0:C], xt_sb[at, s, j].bitcast(F32),
                                            ALU.subtract).then_inc(xt_ready, 1)

            def unit(u, p, first=False, ahead=True):
                maximum(2 * u, 0, 2 * (p % 2))
                if ahead:
                    lo_rows(u + 1, (p + 1) % 2)
                if not (first and p < 2):
                    norm(u - 2, p % 2, start=first)
                maximum(2 * u + 1, 1, 2 * (p % 2) + 1)
                if not (first and p == 0):
                    copy_unit(u - 1, p - 1, 1, start=first and p < 3)

            def transform(c, r, u, base):
                dve.wait_ge(added, u)
                dve.wait_ge(v_lo_done, FREE + base)
                around = image[:, :, bass.ds(r, ROWS + 2), :]
                d = [around[:, :, i:i + ROWS - 1:2, :] for i in range(4)]
                for i, (a, b, op) in enumerate(((0, 2, ALU.subtract), (1, 2, ALU.add), (2, 1, ALU.subtract), (1, 3, ALU.subtract))):
                    nc.vector.tensor_tensor(comp[:, i], d[a], d[b], op).then_inc(comp_done, 1)

            def conv_step(c, q):
                m, k = q // 2, STEPS * c + q
                if q % 2 == 0:
                    dve.wait_ge(m1_done, CT * c + m + 1)
                    nc.vector.tensor_tensor(m12_sum[:], conv_ps[:, 0, 1], m1[:], ALU.add)
                    nc.vector.tensor_tensor(m12_dif[:], m1[:], conv_ps[:, 0, 1], ALU.subtract).then_inc(conv_taken, 1)
                else:
                    dve.wait_ge(conv_done, k + 1)
                    dve.wait_ge(conv_taken, CONV_BANKS + k)
                    dve.wait_ge(relu_done, FREE + CT * c + m)
                    nc.vector.tensor_tensor(y_rows[:, :, 0], conv_ps[:, 1, 0], m12_sum[:], ALU.add)
                    nc.vector.tensor_tensor(y_rows[:, :, 1], m12_dif[:], conv_ps[:, 1, 1], ALU.subtract).then_inc(conv_taken, 1)

            dve.sem_inc(conv_taken, CONV_BANKS)
            dve.wait_ge(pads_ready, 1)

            def first_group(n, conv):
                for p in range(UPG):
                    unit(IMG_UNITS * n + p, p, first=True)
                    if conv:
                        conv_step(GROUPS * n - 1, p)

            def later_groups(n):
                u0 = IMG_UNITS * n
                v0 = u0 + DIR_UNITS
                chunks = GROUPS * n

                def transform_chunk(g):
                    transform(chunks + g, ROWS * g, v0 + UPG * (g + 1) + 1, COMPS * (chunks + g))

                with dve.Fori(1, GROUPS + 1) as g:
                    for p in range(UPG):
                        unit(u0 + UPG * g + p, p)
                for p in range(UPG):
                    unit(v0 + UPG + p, p)
                    if p == 2:
                        transform_chunk(0)

                def row_group(g, last=False):
                    for p in range(UPG):
                        unit(v0 + UPG * g + p, p, ahead=not (last and p == UPG - 1))
                        if p == 2:
                            transform_chunk(g - 1)
                        conv_step(chunks + g - 2, p)

                with dve.Fori(2, GROUPS - 1) as g:
                    row_group(g)
                row_group(GROUPS - 1, last=True)
                last = u0 + IMG_UNITS - 1
                norm(last - 1, 0)
                copy_unit(last, UPG - 1, 1)
                norm(last, 1)
                transform(chunks + GROUPS - 1, ROWS * (GROUPS - 1), last + 1, COMPS * (chunks + GROUPS - 1))

            lo_rows(0, 0)
            first_group(0, conv=False)
            with dve.Fori(0, N - 1) as n:
                later_groups(n)
                for q in range(STEPS):
                    if q == STEPS - 1:
                        lo_rows(IMG_UNITS * (n + 1), 0)
                    conv_step(GROUPS * n + GROUPS - 2, q)
                first_group(n + 1, conv=True)
            later_groups(N - 1)
            for c in (GROUPS - 2, GROUPS - 1):
                for q in range(STEPS):
                    conv_step(GROUPS * (N - 1) + c, q)

        @block.tensor
        def _(pe):
            def sum_cols(k):
                quarters = 2 - k % CT
                for a in range(quarters):
                    pe.wait_ge(sums_in[2 * (k % CT) + a], DMA * (k // CT + 1))
                    if a == 0 and k >= 2:
                        pe.wait_ge(cols_summed, k - 1)
                    blocks = quarter(2 * (k % CT) + a).rearrange("p (b r) w -> p b r w", r=512 // W)
                    for b in range(H // 2 // (512 // W)):
                        first, final = a == b == 0, a == quarters - 1 and b == H // 2 // (512 // W) - 1
                        ins = nc.tensor.matmul(pt_ps[:, k % 2].rearrange("p t (r w) -> p (t r) w", w=W), ident[:], blocks[:, b],
                                               start=first, stop=final)
                    ins.then_inc(cols_read, 1)

            def tables(i):
                for d in range(2):
                    pe.wait_ge(sums_twice, 2 * i + d + 1)
                    if i:
                        pe.wait_ge(y_ready, 2 * (i - 1) + d + 1)
                    for t in range(CT):
                        nc.tensor.matmul(scores[:, d, 0], probs[:, d, t, 0:2 * H], proj[:, d, t], start=t == 0, stop=False)
                    nc.tensor.matmul(scores[:, d, 0], ones_row[:], proj_b[:, d], start=False, stop=True).then_inc(y_psum, 1)

            pe.wait_ge(ident_ready, 1)
            for k in range(CT * N):
                sum_cols(k)
                if k == 2 * CT - 1:
                    pe.wait_ge(small_in, SMALL_LOADS * DMA)
                    pe.wait_ge(ones_ready, 1)
                if k % CT == CT - 1 and k >= 2 * CT - 1:
                    tables(k // CT - 1)
            tables(N - 1)
            pe.wait_ge(w_ready, 1)
            pe.wait_ge(y_ready, 2 * N)

            def transpose_x(u, p, start=False):
                pe.wait_ge(staged, u + 1)
                if not start:
                    pe.wait_ge(xt_ready, 2 * u)
                for t in range(CT):
                    ins = nc.tensor.transpose(xt_ps[:, t * P:(t + 1) * P], st_x[:, p, t, 1:2 * H + 1], ident[:])
                ins.then_inc(xt_done, 1)

            def score(u, p, j, d, start=False):
                pe.wait_ge(xt_ready, 2 * u + j + 1)
                if not start:
                    pe.wait_ge(exp_done, 2 * u + j - 1)
                for t in range(CT):
                    for y, flag in ((y_hi, True), (y_lo, False)):
                        ins = nc.tensor.matmul(scores[:, j, t], xt_sb[:, p % 2, j, t * P:(t + 1) * P],
                                               y[:, d, 2 * p + j], start=flag, stop=not flag)
                ins.then_inc(scored, 1)

            def transpose_p(u, j, start=False):
                pe.wait_ge(exp_done, 2 * u + j + 1)
                if not start:
                    pe.wait_ge(pt_copied[j], u)
                for t in range(CT):
                    for k in range(CT):
                        ins = nc.tensor.transpose(pt_ps[:, j, k, t * P:(t + 1) * P],
                                                  probs[:, j, t, k * P:(k + 1) * P], ident[:])
                ins.then_inc(pt_done, 1)

            def product(u, p, start=False):
                if not start:
                    pe.wait_ge(normed, u)
                for j in range(2):
                    pe.wait_ge(pt_copied[j], u + 1)
                    for t in range(CT):
                        for k in range(CT):
                            half = slice((H + 1) * j, (H + 1) * (j + 1))
                            ins = nc.tensor.matmul(prod_v[:, t, half], probs_t[:, 2 * (p % 2) + j, k, t * P:(t + 1) * P],
                                                   st_x[:, p, k, half], start=k == 0, stop=k == CT - 1)
                ins.then_inc(prod_done, 1)

            def unit(u, p, d, first=False, ahead=True):
                start, before = first and p == 0, not (first and p == 0)
                score(u, p, 0, d, start)
                if before:
                    transpose_p(u - 1, 0, start=first and p == 1)
                if ahead:
                    transpose_x(u + 1, (p + 1) % UPG)
                if not (first and p < 2):
                    product(u - 2, (p - 2) % UPG, start=first and p == 2)
                score(u, p, 1, d, start)
                if before:
                    transpose_p(u - 1, 1, start=first and p == 1)

            def conv_step(c, q, s):
                m, half, k = q // 2, q % 2, STEPS * c + q
                if q == 0:
                    pe.wait_ge(v_lo_done, FREE + COMPS * (c + 1))
                pe.wait_ge(conv_taken, CONV_BANKS + k - 1)
                for b, i in enumerate(STEP_COMPS[half]):
                    parts = [(t, kw, w, v) for t in range(CT) for kw in range(KW)
                             for w, v in ((w_hi, v_hi), (w_hi, v_lo), (w_lo, v_hi))]
                    for a, (t, kw, w, v) in enumerate(parts):
                        ins = nc.tensor.matmul(conv_ps[:, half, b], w[:, t, i, kw, m * P:(m + 1) * P],
                                               v[:, s, i, t, :, kw:kw + W], start=a == 0, stop=a == len(parts) - 1)
                ins.then_inc(conv_done, 1)


            def first_group(n, conv):
                for p in range(UPG):
                    unit(IMG_UNITS * n + p, p, 0, first=True)
                    if conv:
                        conv_step(GROUPS * n - 1, p, (GROUPS - 1) % 2)

            def later_groups(n):
                u0 = IMG_UNITS * n
                v0 = u0 + DIR_UNITS
                chunks = GROUPS * n
                with pe.Fori(1, GROUPS) as g:
                    for p in range(UPG):
                        unit(u0 + UPG * g + p, p, 0)
                with pe.Fori(0, 2) as g:
                    for p in range(UPG):
                        unit(v0 + UPG * g + p, p, 1)

                def row_group(g, s, last=False):
                    for p in range(UPG):
                        unit(v0 + UPG * g + p, p, 1, ahead=not (last and p == UPG - 1))
                        conv_step(chunks + g - 2, p, s)

                with pe.Fori(1, GROUPS // 2 - 1) as h:
                    row_group(2 * h, 0)
                    row_group(2 * h + 1, 1)
                row_group(GROUPS - 2, 0)
                row_group(GROUPS - 1, 1, last=True)
                last = u0 + IMG_UNITS - 1
                product(last - 1, UPG - 2)
                transpose_p(last, 0)
                transpose_p(last, 1)
                product(last, UPG - 1)

            transpose_x(0, 0, start=True)
            first_group(0, conv=False)
            with pe.Fori(0, N - 1) as n:
                later_groups(n)
                for q in range(STEPS):
                    if q == STEPS - 1:
                        transpose_x(IMG_UNITS * (n + 1), 0, start=True)
                    conv_step(GROUPS * n + GROUPS - 2, q, 0)
                first_group(n + 1, conv=True)
            later_groups(N - 1)
            for c in (GROUPS - 2, GROUPS - 1):
                for q in range(STEPS):
                    conv_step(GROUPS * (N - 1) + c, q, c % 2)


def kernel(x, L0_conv_wh, L0_conv_bh, L0_conv_ww, L0_conv_bw, L0_conv_conv_k, L0_conv_bn_w, L0_conv_bn_b,
           L0_conv_bn_mean, L0_conv_bn_var, L0_conv_gamma):
    import concourse.bacc as bacc
    import numpy as np
    from concourse.bass_utils import run_bass_kernel_spmd

    arrays = {
        "x": np.ascontiguousarray(x),
        "wh_t": np.ascontiguousarray(np.asarray(L0_conv_wh).T),
        "bh": np.ascontiguousarray(L0_conv_bh),
        "ww_t": np.ascontiguousarray(np.asarray(L0_conv_ww).T),
        "bw": np.ascontiguousarray(L0_conv_bw),
        "conv_t": np.ascontiguousarray(np.asarray(L0_conv_conv_k).transpose(1, 2, 3, 0)).reshape(C, 3, KW * C),
        "bn_params": np.ascontiguousarray(np.stack([L0_conv_bn_w, L0_conv_bn_b, L0_conv_bn_mean, L0_conv_bn_var])
                                          .reshape(4, CT, P).transpose(2, 0, 1)),
        "gamma": np.ascontiguousarray(L0_conv_gamma),
    }
    nc = bacc.Bacc("TRN2", target_bir_lowering=False, num_devices=1)
    aps = {name: nc.dram_tensor(name, a.shape, mybir.dt.from_np(a.dtype), kind="ExternalInput").ap()
           for name, a in arrays.items()}
    out = nc.dram_tensor("out", (N, C, H, W), F32, kind="ExternalOutput").ap()
    build(nc, **aps, out=out)
    result = run_bass_kernel_spmd(nc, [arrays], core_ids=[0])
    return result.results[0]["out"]
```
